# Optimizing a Trainium2 kernel written in Bass

```python
import numpy as np
import jax
import jax.numpy as jnp

def _softmax(x, axis=-1):
    return jax.nn.softmax(x, axis=axis)

def _gelu(x):
    return jax.nn.gelu(x, approximate=True)

def _silu(x):
    return jax.nn.silu(x)

def _sigmoid(x):
    return jax.nn.sigmoid(x)

def _layernorm(x, axis=-1, eps=1e-05):
    m = jnp.mean(x, axis=axis, keepdims=True)
    v = jnp.var(x, axis=axis, keepdims=True)
    return (x - m) / jnp.sqrt(v + eps)

def _scatter_add(tgt, idx, src, axis=0):
    return tgt.at[idx].add(src)

def _segment_sum(src, seg, n):
    return jax.ops.segment_sum(src, seg, n)
kernel_name = 'mk_dlrm_tower_d1_rec_r8_35020c'

def setup_inputs(seed: int=0):
    np.random.seed(seed)
    _w = jnp.asarray

    def _rec_inputs():
        import jax
        import jax.numpy as jnp
        _tk = jax.random.key(seed)
        dense_ctx = jax.random.normal(jax.random.fold_in(_tk, 190), (512, 16), jnp.float32)
        ids = jnp.stack([jax.random.randint(jax.random.fold_in(_tk, 200 + f), (512,), 0, v, jnp.int32) for f, v in enumerate([12500, 125000, 1000, 12500, 12500, 125000, 1000, 1250, 125000, 1000, 1250, 125000, 12500, 125000, 12500, 1000, 1250, 125000, 1000, 12500, 1250, 12500, 1250, 1000, 1000, 1000, 12500, 1000, 12500, 12500, 1000, 1000, 12500, 1250, 1250, 12500, 12500, 1000, 12500])], axis=1)
        tbl_0 = 0.05 * jax.random.normal(jax.random.fold_in(_tk, 500 + 0), (12500, 32), jnp.float32)
        tbl_1 = 0.05 * jax.random.normal(jax.random.fold_in(_tk, 500 + 1), (125000, 32), jnp.float32)
        tbl_2 = 0.05 * jax.random.normal(jax.random.fold_in(_tk, 500 + 2), (1000, 32), jnp.float32)
        tbl_3 = 0.05 * jax.random.normal(jax.random.fold_in(_tk, 500 + 3), (12500, 32), jnp.float32)
        tbl_4 = 0.05 * jax.random.normal(jax.random.fold_in(_tk, 500 + 4), (12500, 32), jnp.float32)
        tbl_5 = 0.05 * jax.random.normal(jax.random.fold_in(_tk, 500 + 5), (125000, 32), jnp.float32)
        tbl_6 = 0.05 * jax.random.normal(jax.random.fold_in(_tk, 500 + 6), (1000, 32), jnp.float32)
        tbl_7 = 0.05 * jax.random.normal(jax.random.fold_in(_tk, 500 + 7), (1250, 32), jnp.float32)
        tbl_8 = 0.05 * jax.random.normal(jax.random.fold_in(_tk, 500 + 8), (125000, 32), jnp.float32)
        tbl_9 = 0.05 * jax.random.normal(jax.random.fold_in(_tk, 500 + 9), (1000, 32), jnp.float32)
        tbl_10 = 0.05 * jax.random.normal(jax.random.fold_in(_tk, 500 + 10), (1250, 32), jnp.float32)
        tbl_11 = 0.05 * jax.random.normal(jax.random.fold_in(_tk, 500 + 11), (125000, 32), jnp.float32)
        tbl_12 = 0.05 * jax.random.normal(jax.random.fold_in(_tk, 500 + 12), (12500, 32), jnp.float32)
        tbl_13 = 0.05 * jax.random.normal(jax.random.fold_in(_tk, 500 + 13), (125000, 32), jnp.float32)
        tbl_14 = 0.05 * jax.random.normal(jax.random.fold_in(_tk, 500 + 14), (12500, 32), jnp.float32)
        tbl_15 = 0.05 * jax.random.normal(jax.random.fold_in(_tk, 500 + 15), (1000, 32), jnp.float32)
        tbl_16 = 0.05 * jax.random.normal(jax.random.fold_in(_tk, 500 + 16), (1250, 32), jnp.float32)
        tbl_17 = 0.05 * jax.random.normal(jax.random.fold_in(_tk, 500 + 17), (125000, 32), jnp.float32)
        tbl_18 = 0.05 * jax.random.normal(jax.random.fold_in(_tk, 500 + 18), (1000, 32), jnp.float32)
        tbl_19 = 0.05 * jax.random.normal(jax.random.fold_in(_tk, 500 + 19), (12500, 32), jnp.float32)
        tbl_20 = 0.05 * jax.random.normal(jax.random.fold_in(_tk, 500 + 20), (1250, 32), jnp.float32)
        tbl_21 = 0.05 * jax.random.normal(jax.random.fold_in(_tk, 500 + 21), (12500, 32), jnp.float32)
        tbl_22 = 0.05 * jax.random.normal(jax.random.fold_in(_tk, 500 + 22), (1250, 32), jnp.float32)
        tbl_23 = 0.05 * jax.random.normal(jax.random.fold_in(_tk, 500 + 23), (1000, 32), jnp.float32)
        tbl_24 = 0.05 * jax.random.normal(jax.random.fold_in(_tk, 500 + 24), (1000, 32), jnp.float32)
        tbl_25 = 0.05 * jax.random.normal(jax.random.fold_in(_tk, 500 + 25), (1000, 32), jnp.float32)
        tbl_26 = 0.05 * jax.random.normal(jax.random.fold_in(_tk, 500 + 26), (12500, 32), jnp.float32)
        tbl_27 = 0.05 * jax.random.normal(jax.random.fold_in(_tk, 500 + 27), (1000, 32), jnp.float32)
        tbl_28 = 0.05 * jax.random.normal(jax.random.fold_in(_tk, 500 + 28), (12500, 32), jnp.float32)
        tbl_29 = 0.05 * jax.random.normal(jax.random.fold_in(_tk, 500 + 29), (12500, 32), jnp.float32)
        tbl_30 = 0.05 * jax.random.normal(jax.random.fold_in(_tk, 500 + 30), (1000, 32), jnp.float32)
        tbl_31 = 0.05 * jax.random.normal(jax.random.fold_in(_tk, 500 + 31), (1000, 32), jnp.float32)
        tbl_32 = 0.05 * jax.random.normal(jax.random.fold_in(_tk, 500 + 32), (12500, 32), jnp.float32)
        tbl_33 = 0.05 * jax.random.normal(jax.random.fold_in(_tk, 500 + 33), (1250, 32), jnp.float32)
        tbl_34 = 0.05 * jax.random.normal(jax.random.fold_in(_tk, 500 + 34), (1250, 32), jnp.float32)
        tbl_35 = 0.05 * jax.random.normal(jax.random.fold_in(_tk, 500 + 35), (12500, 32), jnp.float32)
        tbl_36 = 0.05 * jax.random.normal(jax.random.fold_in(_tk, 500 + 36), (12500, 32), jnp.float32)
        tbl_37 = 0.05 * jax.random.normal(jax.random.fold_in(_tk, 500 + 37), (1000, 32), jnp.float32)
        tbl_38 = 0.05 * jax.random.normal(jax.random.fold_in(_tk, 500 + 38), (12500, 32), jnp.float32)
        _rk = jax.random.fold_in(_tk, 7)
        W_top1 = 0.0363456 * jax.random.normal(jax.random.fold_in(_tk, 801), (757, 512), jnp.float32)
        W_top2 = 0.0441942 * jax.random.normal(jax.random.fold_in(_tk, 802), (512, 256), jnp.float32)
        W_top3 = 0.0625 * jax.random.normal(jax.random.fold_in(_tk, 803), (256, 1), jnp.float32)
        b_top1 = jnp.zeros((512,), jnp.float32)
        b_top2 = jnp.zeros((256,), jnp.float32)
        return (dense_ctx, ids, tbl_0, tbl_1, tbl_2, tbl_3, tbl_4, tbl_5, tbl_6, tbl_7, tbl_8, tbl_9, tbl_10, tbl_11, tbl_12, tbl_13, tbl_14, tbl_15, tbl_16, tbl_17, tbl_18, tbl_19, tbl_20, tbl_21, tbl_22, tbl_23, tbl_24, tbl_25, tbl_26, tbl_27, tbl_28, tbl_29, tbl_30, tbl_31, tbl_32, tbl_33, tbl_34, tbl_35, tbl_36, tbl_37, tbl_38, W_top1, b_top1, W_top2, b_top2, W_top3)
    dense_ctx, ids, tbl_0, tbl_1, tbl_2, tbl_3, tbl_4, tbl_5, tbl_6, tbl_7, tbl_8, tbl_9, tbl_10, tbl_11, tbl_12, tbl_13, tbl_14, tbl_15, tbl_16, tbl_17, tbl_18, tbl_19, tbl_20, tbl_21, tbl_22, tbl_23, tbl_24, tbl_25, tbl_26, tbl_27, tbl_28, tbl_29, tbl_30, tbl_31, tbl_32, tbl_33, tbl_34, tbl_35, tbl_36, tbl_37, tbl_38, W_top1, b_top1, W_top2, b_top2, W_top3 = _rec_inputs()

    def _L0_rec_setup():
        import jax, jax.numpy as jnp
        import numpy as np
        F = 39

        def _pair_indices(f):
            row, col = ([], [])
            for i in range(f - 1):
                for j in range(i + 1, f):
                    row.append(i)
                    col.append(j)
            return (np.array(row, np.int32), np.array(col, np.int32))
        ROW, COL = _pair_indices(F)
        key = jax.random.key(seed)
        k1, k2 = jax.random.split(key)
        B, k = (1024, 32)
        P = F * (F - 1) // 2
        inputs = jax.random.normal(k1, (B, F, k), dtype=jnp.float32)
        w = jax.random.normal(k2, (k, P, k), dtype=jnp.float32)
        return {'inputs': inputs, 'w': w}
    _L0_rec_all = _L0_rec_setup()
    _L0_rec_in = {k: v for k, v in _L0_rec_all.items() if k in ('w',)}
    del _L0_rec_all
    return {'dense_ctx': dense_ctx, 'ids': ids, 'tbl_0': tbl_0, 'tbl_1': tbl_1, 'tbl_2': tbl_2, 'tbl_3': tbl_3, 'tbl_4': tbl_4, 'tbl_5': tbl_5, 'tbl_6': tbl_6, 'tbl_7': tbl_7, 'tbl_8': tbl_8, 'tbl_9': tbl_9, 'tbl_10': tbl_10, 'tbl_11': tbl_11, 'tbl_12': tbl_12, 'tbl_13': tbl_13, 'tbl_14': tbl_14, 'tbl_15': tbl_15, 'tbl_16': tbl_16, 'tbl_17': tbl_17, 'tbl_18': tbl_18, 'tbl_19': tbl_19, 'tbl_20': tbl_20, 'tbl_21': tbl_21, 'tbl_22': tbl_22, 'tbl_23': tbl_23, 'tbl_24': tbl_24, 'tbl_25': tbl_25, 'tbl_26': tbl_26, 'tbl_27': tbl_27, 'tbl_28': tbl_28, 'tbl_29': tbl_29, 'tbl_30': tbl_30, 'tbl_31': tbl_31, 'tbl_32': tbl_32, 'tbl_33': tbl_33, 'tbl_34': tbl_34, 'tbl_35': tbl_35, 'tbl_36': tbl_36, 'tbl_37': tbl_37, 'tbl_38': tbl_38, 'W_top1': W_top1, 'b_top1': b_top1, 'W_top2': W_top2, 'b_top2': b_top2, 'W_top3': W_top3, 'L0_rec_w': _L0_rec_in['w']}

def reference(dense_ctx, ids, tbl_0, tbl_1, tbl_2, tbl_3, tbl_4, tbl_5, tbl_6, tbl_7, tbl_8, tbl_9, tbl_10, tbl_11, tbl_12, tbl_13, tbl_14, tbl_15, tbl_16, tbl_17, tbl_18, tbl_19, tbl_20, tbl_21, tbl_22, tbl_23, tbl_24, tbl_25, tbl_26, tbl_27, tbl_28, tbl_29, tbl_30, tbl_31, tbl_32, tbl_33, tbl_34, tbl_35, tbl_36, tbl_37, tbl_38, W_top1, b_top1, W_top2, b_top2, W_top3, L0_rec_w):
    import jax
    import jax.numpy as jnp

    def _L0_rec_ref(inputs, w):
        import jax, jax.numpy as jnp
        import numpy as np
        F = 39

        def _pair_indices(f):
            row, col = ([], [])
            for i in range(f - 1):
                for j in range(i + 1, f):
                    row.append(i)
                    col.append(j)
            return (np.array(row, np.int32), np.array(col, np.int32))
        ROW, COL = _pair_indices(F)
        p = inputs[:, ROW, :]
        q = inputs[:, COL, :]
        return jnp.einsum('bpc,apc,bpa->bp', p, w, q)
    e = jnp.stack([tbl_0[ids[:, 0]], tbl_1[ids[:, 1]], tbl_2[ids[:, 2]], tbl_3[ids[:, 3]], tbl_4[ids[:, 4]], tbl_5[ids[:, 5]], tbl_6[ids[:, 6]], tbl_7[ids[:, 7]], tbl_8[ids[:, 8]], tbl_9[ids[:, 9]], tbl_10[ids[:, 10]], tbl_11[ids[:, 11]], tbl_12[ids[:, 12]], tbl_13[ids[:, 13]], tbl_14[ids[:, 14]], tbl_15[ids[:, 15]], tbl_16[ids[:, 16]], tbl_17[ids[:, 17]], tbl_18[ids[:, 18]], tbl_19[ids[:, 19]], tbl_20[ids[:, 20]], tbl_21[ids[:, 21]], tbl_22[ids[:, 22]], tbl_23[ids[:, 23]], tbl_24[ids[:, 24]], tbl_25[ids[:, 25]], tbl_26[ids[:, 26]], tbl_27[ids[:, 27]], tbl_28[ids[:, 28]], tbl_29[ids[:, 29]], tbl_30[ids[:, 30]], tbl_31[ids[:, 31]], tbl_32[ids[:, 32]], tbl_33[ids[:, 33]], tbl_34[ids[:, 34]], tbl_35[ids[:, 35]], tbl_36[ids[:, 36]], tbl_37[ids[:, 37]], tbl_38[ids[:, 38]]], axis=1)
    z = _L0_rec_ref(e, L0_rec_w)
    z = z.reshape(z.shape[0], -1)
    h = jnp.concatenate([z, dense_ctx], axis=1)
    h = jnp.maximum(h @ W_top1 + b_top1, 0.0)
    h = jnp.maximum(h @ W_top2 + b_top2, 0.0)
    y = h @ W_top3
    return y

_drawn_inputs = setup_inputs


def setup_inputs(seed=0):
    import zlib

    import numpy as np

    out = dict(_drawn_inputs(seed))
    spreads = {'b_top1': (0.0, 0.1), 'b_top2': (0.0, 0.1)}
    factors = {}
    for name, (base, spread) in spreads.items():
        noise = np.random.default_rng([zlib.crc32(name.encode()), seed]).standard_normal(out[name].shape)
        drawn = base * np.exp(spread * noise) if base else spread * noise
        out[name] = jnp.asarray(drawn.astype(out[name].dtype))
    for name, factor in factors.items():
        out[name] = (out[name] * factor).astype(out[name].dtype)
    return out
```

```python
from contextlib import ExitStack

import numpy as np

import concourse.bass as bass
from concourse import mybir

ALU = mybir.AluOpType
ACT = mybir.ActivationFunctionType
F32 = mybir.dt.float32
F32R = mybir.dt.float32r
I32 = mybir.dt.int32

P = 128
F = 39
K = 32
B = 512
NCHUNK = B // P
G = P // K
NBLK = -(-F // G)
NDENSE = 16
H1, H2 = 512, 256
M1, M2 = H1 // P, H2 // P

ORDER = list(range(F))

GROUP = 3
XSLOTS = 4
WCHUNK = 14
WSLOTS = 3
ZTILES = P // G
ZM = ZTILES // G


def in_block(J):
    return min(G, F - G * J)


def make_schedule():
    groups = []
    for J in range(NBLK):
        n = in_block(J)
        src = [G * J + r for r in range(n)]
        every = list(range(G))
        whole = J - J % GROUP
        for s in src:
            for I0 in range(0, whole, GROUP):
                groups.append((J, I0, GROUP, [[(s, every)]] * GROUP))
        for I in range(whole, J):
            groups.append((J, I, 1, [[(s, every)] for s in src[:GROUP]]))
        if n > GROUP and J > whole:
            groups.append((J, whole, J - whole, [[(src[GROUP], every)]] * (J - whole)))
        s = src
        if n == 4:
            groups.append((J, J, 1, [[(s[2], [0]), (s[0], [1]), (s[1], [2, 3])], [(s[3], [0, 2])]]))
        else:
            groups.append((J, J, 1, [[(s[2], [0]), (s[0], [1]), (s[1], [2])]]))
    return groups


GROUPS = make_schedule()
NGROUP = len(GROUPS)
TILE_BASE = [0]
PASS_BASE = [0]
for _g in GROUPS:
    TILE_BASE.append(TILE_BASE[-1] + len(_g[3]))
    PASS_BASE.append(PASS_BASE[-1] + sum(len(t) for t in _g[3]))
NTILE, NPASS = TILE_BASE[-1], PASS_BASE[-1]
NZ = -(-NTILE // ZTILES)
NWCHUNK = -(-NPASS // WCHUNK)
WCOLS = WCHUNK * P
NWCOL = -(-NWCHUNK // G)
GROUP_OF_TILE = [g for g in range(NGROUP) for _ in GROUPS[g][3]]
LAST_GROUP = [max(g for g in range(NGROUP) if GROUPS[g][0] == J) for J in range(NBLK)]
FIRST_GROUP = [min(g for g in range(NGROUP) if GROUPS[g][0] == J) for J in range(NBLK)]
EARLY_Z = 4
SEL_LAG = 2


def plan():
    steps, done, summed_z = [], 0, 0
    early = None

    def sums(upto, exact):
        nonlocal done, early
        end = TILE_BASE[upto + 1] if upto >= 0 else 0
        while done < end and (exact or end - done >= G - done % G):
            n = min(G - done % G, end - done)
            steps.append(("sums", done, n))
            done += n
            if done % ZTILES == 0 or done == NTILE:
                steps.append(("z", (done - 1) // ZTILES, sum(s[0] == "sums" for s in steps)))
                if (done - 1) // ZTILES == EARLY_Z - 1:
                    early = 0

    wait = 0
    for J in range(NBLK):
        steps.append(("turn", J))
        for g in range(FIRST_GROUP[J], LAST_GROUP[J] + 1):
            steps.append(("tiles", g))
            sums(g - SEL_LAG, False)
            sums(g - XSLOTS + 1, True)
            if early is not None and early < M1:
                wait += 1
                if wait % 3 == 0:
                    steps.append(("early", early))
                    early += 1
    sums(NGROUP - 1, True)
    while early < M1:
        steps.append(("early", early))
        early += 1
    return steps


PLAN = plan()


def pair_of(a, b):
    i, j = min(a, b), max(a, b)
    return i * (2 * F - i - 1) // 2 + (j - i - 1)


def lay_out_weights(w, W_top1):
    wst = np.zeros((NWCOL, G, K, WCHUNK, G, K), w.dtype)
    w1 = np.zeros((NZ * P, H1), W_top1.dtype)
    n = 0
    for g, (J, I0, nI, tiles) in enumerate(GROUPS):
        for i, tile in enumerate(tiles):
            I = I0 + i if nI > 1 else I0
            t = TILE_BASE[g] + i
            for src, rows in tile:
                c, at = n // WCHUNK, n % WCHUNK
                for r in rows:
                    a, b = ORDER[src], ORDER[G * I + r]
                    block = w[:, pair_of(a, b), :]
                    wst[c // G, c % G, :, at, r, :] = block if a > b else block.T
                    z = (t // ZTILES) * P + (t % G) * K + (t % ZTILES // G) * G + r
                    w1[z] = W_top1[pair_of(a, b)]
                n += 1
    return wst.reshape(NWCOL, P, WCOLS), w1


def dlrm_tower(nc, tables, ids, dense_t, wst, w1, w1d, w2, columns, y):
    with ExitStack() as ctx:
        def sb(name, shape, dt=F32):
            return ctx.enter_context(nc.sbuf_tensor(name, shape, dt))

        def sem(name):
            return ctx.enter_context(nc.semaphore(name))

        ids_sb = sb("ids_sb", [P, NCHUNK * F], I32)
        ident = sb("ident", [P, P])
        sel = sb("sel", [P, ZM, K])
        gathered = sb("gathered", [P, 3, NCHUNK, P])
        eT = sb("eT", [P, NBLK, B])
        e_hi = sb("e_hi", [P, 2, B])
        e_lo = sb("e_lo", [P, 2, B])
        stack = sb("stack", [P, 2, G, B])
        w_lo = sb("w_lo", [P, NWCOL, WCOLS])
        w_hi = sb("w_hi", [P, NWCOL, WCOLS])
        wring = sb("wring", [P, WSLOTS, WCHUNK, P])
        prod = sb("prod", [P, XSLOTS, GROUP, B])
        z_sb = sb("z_sb", [P, NZ, B])
        dense_sb = sb("dense_sb", [NDENSE, B])
        w1_sb = sb("w1_sb", [P, NZ, H1])
        w1d_sb = sb("w1d_sb", [NDENSE, H1])
        w2_sb = sb("w2_sb", [P, M1, H2])
        columns_sb = sb("columns_sb", [P, M1 + 2 * M2])
        b1_sb = columns_sb[:, 0:M1]
        b2_sb = columns_sb[:, M1:M1 + M2]
        w3_sb = columns_sb[:, M1 + M2:]
        h_early = sb("h_early", [P, M1, B])
        y_sb = sb("y_sb", [1, B])
        h1_sum = [prod[:, 0, m, :] if m < GROUP else prod[:, 1, 0, :] for m in range(M1)]
        h1_sb = [prod[:, 2, m, :] if m < GROUP else prod[:, 1, 1, :] for m in range(M1)]
        h2_sb = [prod[:, 3, m, :] for m in range(M2)]

        t_ps = [ctx.enter_context(nc.psum_tensor(f"t_ps{i}", [P, GROUP, B], F32)) for i in range(2)]
        z_ps = ctx.enter_context(nc.psum_tensor("z_ps", [P, B], F32))
        side_ps = ctx.enter_context(nc.psum_tensor("side_ps", [P, B], F32))
        h1_ps = [t_ps[0][:, 0, :], t_ps[0][:, 1, :], t_ps[0][:, 2, :], t_ps[1][:, 0, :]]
        h2_ps = [t_ps[1][:, 1, :], t_ps[1][:, 2, :]]
        y_ps = side_ps[0:1, :]

        ids_in = sem("ids_in")
        w_in = [sem(f"w_in{c}") for c in range(NWCOL)]
        mlp_in = sem("mlp_in")
        consts_zero = sem("consts_zero")
        consts_made = sem("consts_made")
        pad_zeroed = sem("pad_zeroed")
        rows_in = [sem(f"rows_in{J}") for J in range(NBLK)]
        turned = sem("turned")
        eT_made = sem("eT_made")
        e_hi_made = sem("e_hi_made")
        e_lo_made = sem("e_lo_made")
        stack_in = [sem(f"stack_in{J}") for J in range(NBLK)]
        w_hi_made = sem("w_hi_made")
        w_lo_made = sem("w_lo_made")
        wring_in = [sem(f"wring_in{i}") for i in range(WSLOTS)]
        tiles_made = sem("tiles_made")
        multiplied = sem("multiplied")
        summed = sem("summed")
        z_kept = sem("z_kept")
        early_made = sem("early_made")
        early_kept = sem("early_kept")
        h1_made = sem("h1_made")
        h1_added = sem("h1_added")
        h1_kept = sem("h1_kept")
        h2_made = sem("h2_made")
        h2_kept = sem("h2_kept")
        y_made = sem("y_made")
        y_kept = sem("y_kept")
        y_out = sem("y_out")

        mlp_loads = [(w1_sb[:, :, :], w1.rearrange("(k p) n -> p k n", p=P)),
                     (w1d_sb[:, :], w1d), (dense_sb[:, :], dense_t),
                     (w2_sb[:, :, :], w2.rearrange("(k p) n -> p k n", p=P)),
                     (columns_sb[:, :], columns)]
        sums = [s for s in PLAN if s[0] == "sums"]
        sums_through = [next(i + 1 for i, s in enumerate(sums) if s[1] + s[2] >= TILE_BASE[g + 1])
                        for g in range(NGROUP)]
        chunk_last_group = [next(g for g in range(NGROUP)
                                 if PASS_BASE[g + 1] >= min(NPASS, (c + 1) * WCHUNK))
                            for c in range(NWCHUNK)]

        block = ctx.enter_context(nc.Block())

        @block.sync
        def _(sp):
            sp.dma_start(ids_sb[:, :], ids).then_inc(ids_in, 16)
            for c in range(NWCOL):
                sp.dma_start(w_lo[:, c, :], wst[c, :, :]).then_inc(w_in[c], 16)
            for dst, src in mlp_loads:
                sp.dma_start(dst, src).then_inc(mlp_in, 16)

            def fill_ring(c):
                sp.wait_ge(w_hi_made, c // G + 1)
                sp.wait_ge(w_lo_made, c // G + 1)
                if c >= WSLOTS:
                    sp.wait_ge(tiles_made, chunk_last_group[c - WSLOTS] + 1)
                q = K * (c % G)
                for i, part in enumerate((w_hi, w_lo, w_hi, w_lo)):
                    sp.dma_start(wring[K * i:K * i + K, c % WSLOTS, :, :].rearrange("p a b -> p (a b)"),
                                 part[q:q + K, c // G, :]).then_inc(wring_in[c % WSLOTS], 16)

            c = 0
            for J in range(NBLK):
                while c < NWCHUNK and (c < WSLOTS or chunk_last_group[c - WSLOTS] < FIRST_GROUP[J]):
                    fill_ring(c)
                    c += 1
                sp.wait_ge(e_lo_made, J + 1)
                if J >= 2:
                    sp.wait_ge(tiles_made, LAST_GROUP[J - 2] + 1)
                for r in range(in_block(J)):
                    for i in (2, 3):
                        sp.dma_start(stack[K * i:K * i + K, J % 2, r, :],
                                     e_lo[K * r:K * r + K, J % 2, :]).then_inc(stack_in[J], 16)
            while c < NWCHUNK:
                fill_ring(c)
                c += 1
            sp.wait_ge(y_kept, 1)
            sp.dma_start(y.rearrange("b o -> o b"), y_sb[:, :]).then_inc(y_out, 16)
            sp.wait_ge(y_out, 16)

        @block.gpsimd
        def _(pool):
            pool.memset(ident[:, :], 0.0).then_inc(consts_zero, 1)
            pool.memset(sel[:, :, :], 1.0).then_inc(consts_zero, 1)
            pool.wait_ge(consts_zero, 2)
            pool.affine_select(out=ident[:, :], in_=ident[:, :], compare_op=ALU.not_equal, fill=1.0, base=0,
                               pattern=[[-1, P]], channel_multiplier=1).then_inc(consts_made, 1)
            pool.affine_select(out=sel[:, :, :], in_=sel[:, :, :], compare_op=ALU.is_ge, fill=0.0, base=0,
                               pattern=[[P, ZM], [-K, K]], channel_multiplier=1).then_inc(consts_made, 1)
            pool.wait_ge(consts_made, 2)
            pool.affine_select(out=sel[:, :, :], in_=sel[:, :, :], compare_op=ALU.is_ge, fill=0.0, base=K - 1,
                               pattern=[[-P, ZM], [K, K]], channel_multiplier=-1).then_inc(consts_made, 1)
            pool.wait_ge(ids_in, 16)
            for J in range(NBLK):
                if J >= 3:
                    pool.wait_ge(turned, J - 2)
                for r in range(in_block(J)):
                    f = ORDER[G * J + r]
                    for b in range(NCHUNK):
                        pool.indirect_dma_start(
                            gathered[:, J % 3, b, K * r:K * r + K], None, tables[f],
                            bass.IndirectOffsetOnAxis(ap=ids_sb[:, F * b + f:F * b + f + 1], axis=0),
                        ).then_inc(rows_in[J], 16)

        @block.scalar
        def _(act):
            for c in range(NWCOL):
                act.wait_ge(w_in[c], 16)
                act.activation(w_hi[:, c, :].bitcast(F32R), w_lo[:, c, :], ACT.Copy).then_inc(w_hi_made, 1)
            for step in PLAN:
                if step[0] == "turn":
                    J = step[1]
                    n = K * in_block(J)
                    act.wait_ge(turned, J + 1)
                    act.activation(eT[0:n, J, :], side_ps[0:n, :], ACT.Copy).then_inc(eT_made, 1)
                    if J >= 2:
                        act.wait_ge(stack_in[J - 2], 16 * G * G)
                    act.activation(e_hi[0:n, J % 2, :].bitcast(F32R), side_ps[0:n, :],
                                   ACT.Copy).then_inc(e_hi_made, 1)
                    act.wait_ge(e_hi_made, J + 1)
                    if J >= 2:
                        act.wait_ge(tiles_made, LAST_GROUP[J - 2] + 1)
                    for r in range(in_block(J)):
                        for i in (0, 1):
                            act.dma_start(stack[K * i:K * i + K, J % 2, r, :],
                                          e_hi[K * r:K * r + K, J % 2, :]).then_inc(stack_in[J], 16)
                elif step[0] == "z":
                    act.wait_ge(summed, step[2])
                    act.activation(z_sb[:, step[1], :], z_ps[:, :], ACT.Copy).then_inc(z_kept, 1)
                elif step[0] == "early":
                    m = step[1]
                    if m == 0:
                        act.wait_ge(mlp_in, 16 * len(mlp_loads))
                    act.wait_ge(early_made, m + 1)
                    act.activation(h_early[:, m, :], side_ps[:, :], ACT.Identity,
                                   bias=b1_sb[:, m:m + 1]).then_inc(early_kept, 1)
            for m in range(M1):
                act.wait_ge(h1_added, m + 1)
                act.activation(h1_sb[m], h1_sum[m], ACT.Relu).then_inc(h1_kept, 1)
            for m in range(M2):
                act.wait_ge(h2_made, m + 1)
                act.activation(h2_sb[m], h2_ps[m], ACT.Relu, bias=b2_sb[:, m:m + 1]).then_inc(h2_kept, 1)
            act.wait_ge(y_made, 1)
            act.activation(y_sb[:, :], y_ps, ACT.Copy).then_inc(y_kept, 1)

        @block.vector
        def _(dve):
            last = in_block(NBLK - 1) * K
            dve.memset(eT[last:P, NBLK - 1, :], 0.0).then_inc(pad_zeroed, 1)
            for c in range(NWCOL):
                dve.wait_ge(w_hi_made, c + 1)
                dve.tensor_tensor(w_lo[:, c, :].bitcast(F32R), w_lo[:, c, :], w_hi[:, c, :],
                                  ALU.subtract).then_inc(w_lo_made, 1)
            dve.wait_ge(pad_zeroed, 1)
            for step in PLAN:
                if step[0] == "turn":
                    J = step[1]
                    n = K * in_block(J)
                    dve.wait_ge(eT_made, J + 1)
                    dve.wait_ge(e_hi_made, J + 1)
                    if J >= 2:
                        dve.wait_ge(stack_in[J - 2], 16 * G * G)
                    dve.tensor_tensor(e_lo[0:n, J % 2, :].bitcast(F32R), eT[0:n, J, :], e_hi[0:n, J % 2, :],
                                      ALU.subtract).then_inc(e_lo_made, 1)
                elif step[0] == "tiles":
                    g = step[1]
                    J, I0, nI, tiles = GROUPS[g]
                    n = len(tiles)
                    dve.wait_ge(tiles_made, g + 1)
                    if g >= XSLOTS:
                        dve.wait_ge(summed, sums_through[g - XSLOTS])
                    if nI > 1:
                        field = eT[:, I0:I0 + n, :]
                    else:
                        field = eT[:, I0:I0 + 1, :].broadcast_to([P, n, B])
                    dve.tensor_tensor(prod[:, g % XSLOTS, 0:n, :], t_ps[g % 2][:, 0:n, :], field,
                                      ALU.mult).then_inc(multiplied, 1)
            for m in range(M1):
                dve.wait_ge(h1_made, m + 1)
                dve.wait_ge(early_kept, m + 1)
                if m == 0:
                    dve.wait_ge(summed, len(sums))
                dve.tensor_tensor(h1_sum[m], h1_ps[m], h_early[:, m, :], ALU.add).then_inc(h1_added, 1)

        @block.tensor
        def _(pe):
            passes = 0
            side_used = []

            def side_free():
                if side_used:
                    pe.wait_ge(*side_used[-1])

            for step in PLAN:
                if step[0] == "turn":
                    J = step[1]
                    n = K * in_block(J)
                    if J == 0:
                        pe.wait_ge(consts_made, 3)
                    pe.wait_ge(rows_in[J], 16 * in_block(J) * NCHUNK)
                    side_free()
                    for b in range(NCHUNK):
                        mm = pe.transpose(side_ps[0:n, P * b:P * b + P], gathered[:, J % 3, b, 0:n], ident[:, :])
                    mm.then_inc(turned, 1)
                    side_used.append((e_hi_made, J + 1))
                elif step[0] == "tiles":
                    g = step[1]
                    J, I0, nI, tiles = GROUPS[g]
                    if g == FIRST_GROUP[J]:
                        pe.wait_ge(stack_in[J], 16 * in_block(J) * G)
                    if g >= 2:
                        pe.wait_ge(multiplied, g - 1)
                    for i, tile in enumerate(tiles):
                        for k, (src, _) in enumerate(tile):
                            c = passes // WCHUNK
                            if passes % WCHUNK == 0:
                                pe.wait_ge(wring_in[c % WSLOTS], 16 * G * (c // WSLOTS + 1))
                            mm = pe.matmul(t_ps[g % 2][:, i, :],
                                           wring[:, c % WSLOTS, passes % WCHUNK, :].bitcast(F32R),
                                           stack[:, J % 2, src - G * J, :].bitcast(F32R),
                                           start=(k == 0), stop=(k == len(tile) - 1))
                            passes += 1
                    mm.then_inc(tiles_made, 1)
                elif step[0] == "sums":
                    for t in range(step[1], step[1] + step[2]):
                        g = GROUP_OF_TILE[t]
                        u = t % ZTILES
                        if t == step[1] or g != GROUP_OF_TILE[t - 1]:
                            pe.wait_ge(multiplied, g + 1)
                        if u == 0 and t > 0:
                            pe.wait_ge(z_kept, t // ZTILES)
                        mm = pe.matmul(z_ps[K * (u % G):K * (u % G) + K, :], sel[:, u // G, :],
                                       prod[:, g % XSLOTS, t - TILE_BASE[g], :],
                                       start=(u < G), stop=(u >= ZTILES - G or t >= NTILE - G))
                    mm.then_inc(summed, 1)
                elif step[0] == "early":
                    m = step[1]
                    if m == 0:
                        pe.wait_ge(mlp_in, 16 * len(mlp_loads))
                        pe.wait_ge(z_kept, EARLY_Z)
                    side_free()
                    cols = slice(P * m, P * m + P)
                    pe.matmul(side_ps[:, :], w1d_sb[:, cols], dense_sb[:, :], start=True, stop=False)
                    for zb in range(EARLY_Z):
                        mm = pe.matmul(side_ps[:, :], w1_sb[:, zb, cols], z_sb[:, zb, :],
                                       start=False, stop=(zb == EARLY_Z - 1))
                    mm.then_inc(early_made, 1)
                    side_used.append((early_kept, m + 1))
            pe.wait_ge(multiplied, NGROUP)
            for m in range(M1):
                for zb in range(EARLY_Z, NZ):
                    pe.wait_ge(z_kept, zb + 1)
                    mm = pe.matmul(h1_ps[m], w1_sb[:, zb, P * m:P * m + P], z_sb[:, zb, :],
                                   start=(zb == EARLY_Z), stop=(zb == NZ - 1))
                mm.then_inc(h1_made, 1)
            for k in range(M1):
                pe.wait_ge(h1_kept, k + 1)
                for m in range(M2):
                    mm = pe.matmul(h2_ps[m], w2_sb[:, k, P * m:P * m + P], h1_sb[k],
                                   start=(k == 0), stop=(k == M1 - 1))
                    if k == M1 - 1:
                        mm.then_inc(h2_made, 1)
            side_free()
            for k in range(M2):
                pe.wait_ge(h2_kept, k + 1)
                mm = pe.matmul(y_ps, w3_sb[:, k:k + 1], h2_sb[k], start=(k == 0), stop=(k == M2 - 1))
            mm.then_inc(y_made, 1)


def kernel(**inputs):
    import concourse.bacc as bacc
    from concourse.bass_utils import run_bass_kernel_spmd

    a = {k: np.asarray(v) for k, v in inputs.items()}
    wst, w1 = lay_out_weights(a["L0_rec_w"], a["W_top1"])
    arrays = {f"tbl_{f}": np.ascontiguousarray(a[f"tbl_{f}"]) for f in range(F)}
    arrays["ids"] = np.ascontiguousarray(a["ids"].reshape(NCHUNK, P, F).transpose(1, 0, 2).reshape(P, -1))
    arrays["dense_t"] = np.ascontiguousarray(a["dense_ctx"].T)
    arrays["wst"], arrays["w1"] = wst, w1
    arrays["w1d"] = np.ascontiguousarray(a["W_top1"][F * (F - 1) // 2:])
    arrays["w2"] = np.ascontiguousarray(a["W_top2"])
    arrays["columns"] = np.concatenate(
        [a[n].reshape(-1, P).T for n in ("b_top1", "b_top2", "W_top3")], axis=1)

    nc = bacc.Bacc("TRN2", target_bir_lowering=False, num_devices=1)
    ap = {name: nc.dram_tensor(name, v.shape, mybir.dt.from_np(v.dtype), kind="ExternalInput").ap()
          for name, v in arrays.items()}
    y = nc.dram_tensor("y", (B, 1), F32, kind="ExternalOutput").ap()
    dlrm_tower(nc, [ap[f"tbl_{f}"] for f in range(F)],
               *(ap[n] for n in ("ids", "dense_t", "wst", "w1", "w1d", "w2", "columns")), y)
    r = run_bass_kernel_spmd(nc, [arrays], core_ids=[0])
    return r.results[0]["y"]
```

```python
from contextlib import ExitStack

import numpy as np

import concourse.bass as bass
from concourse import mybir

ALU = mybir.AluOpType
ACT = mybir.ActivationFunctionType
BF16 = mybir.dt.bfloat16
F16 = mybir.dt.float16
F32 = mybir.dt.float32
F32R = mybir.dt.float32r
I32 = mybir.dt.int32

P = 128
F = 39
K = 32
B = 512
NCHUNK = B // P
G = P // K
NBLK = -(-F // G)
NDENSE = 16
H1, H2 = 512, 256
M1, M2 = H1 // P, H2 // P

TABLE_ROWS = [12500, 125000, 1000, 12500, 12500, 125000, 1000, 1250, 125000, 1000, 1250, 125000, 12500,
              125000, 12500, 1000, 1250, 125000, 1000, 12500, 1250, 12500, 1250, 1000, 1000, 1000, 12500,
              1000, 12500, 12500, 1000, 1000, 12500, 1250, 1250, 12500, 12500, 1000, 12500]
NHOT = 3
HOT_ROWS = 1000
NSLICE = 8
HP = HOT_ROWS // NSLICE
HOT_BUFS = 3
HOT_FIELDS = [f for f in range(F) if TABLE_ROWS[f] == HOT_ROWS][:G * NHOT]
ORDER = HOT_FIELDS + [f for f in range(F) if f not in HOT_FIELDS]

GROUP = 3
XSLOTS = 4
WCHUNK = 14
WSLOTS = 2
ZTILES = P // G
ZM = ZTILES // G


def in_block(J):
    return min(G, F - G * J)


def make_schedule():
    groups = []
    for J in range(NBLK):
        n = in_block(J)
        src = [G * J + r for r in range(n)]
        every = list(range(G))
        whole = J - J % GROUP
        for s in src:
            for I0 in range(0, whole, GROUP):
                groups.append((J, I0, GROUP, [[(s, every)]] * GROUP))
        for I in range(whole, J):
            groups.append((J, I, 1, [[(s, every)] for s in src[:GROUP]]))
        if n > GROUP and J > whole:
            groups.append((J, whole, J - whole, [[(src[GROUP], every)]] * (J - whole)))
        s = src
        if n == 4:
            groups.append((J, J, 1, [[(s[2], [0]), (s[0], [1]), (s[1], [2, 3])], [(s[3], [0, 2])]]))
        else:
            groups.append((J, J, 1, [[(s[2], [0]), (s[0], [1]), (s[1], [2])]]))
    return groups


GROUPS = make_schedule()
NGROUP = len(GROUPS)
TILE_BASE = [0]
PASS_BASE = [0]
for _g in GROUPS:
    TILE_BASE.append(TILE_BASE[-1] + len(_g[3]))
    PASS_BASE.append(PASS_BASE[-1] + sum(len(t) for t in _g[3]))
NTILE, NPASS = TILE_BASE[-1], PASS_BASE[-1]
NZ = -(-NTILE // ZTILES)
NWCHUNK = -(-NPASS // WCHUNK)
WCOLS = WCHUNK * P
NWCOL = -(-NWCHUNK // G)
GROUP_OF_TILE = [g for g in range(NGROUP) for _ in GROUPS[g][3]]
LAST_GROUP = [max(g for g in range(NGROUP) if GROUPS[g][0] == J) for J in range(NBLK)]
FIRST_GROUP = [min(g for g in range(NGROUP) if GROUPS[g][0] == J) for J in range(NBLK)]
EARLY_Z = 4
SEL_LAG = 2


def plan():
    steps, done, early = [], 0, None

    def sums(upto, exact):
        nonlocal done, early
        end = TILE_BASE[upto + 1] if upto >= 0 else 0
        while done < end and (exact or end - done >= G - done % G):
            n = min(G - done % G, end - done)
            steps.append(("sums", done, n))
            done += n
            if done % ZTILES == 0 or done == NTILE:
                zb = (done - 1) // ZTILES
                steps.append(("z", zb, sum(s[0] == "sums" for s in steps)))
                if zb == EARLY_Z - 1:
                    early = 0

    def turn(J):
        return [("keep", J), ("halve", J)] + [("lift", J, r) for r in range(in_block(J))]

    half = NSLICE // 2
    lifts = [turn(J)[2:] for J in range(NHOT)]
    steps += [("split", 0, 0), ("ids", 0), ("split", 0, 1), ("split", 1, 0), ("look", 0, 0, half), ("ids", 1),
              ("split", 1, 1), ("look", 0, half, NSLICE), ("split", 2, 0), ("w", 0), ("look", 1, 0, half),
              ("keep", 0), ("split", 2, 1), ("ids", 2), ("look", 1, half, NSLICE), ("halve", 0),
              ("look", 2, 0, half), ("keep", 1), *lifts[0], ("look", 2, half, NSLICE),
              ("halve", 1), ("w", 1), ("keep", 2), *lifts[1]]
    for J in range(NBLK):
        coming = turn(J + 1) if 2 <= J < NBLK - 1 else []
        for g in range(FIRST_GROUP[J], LAST_GROUP[J] + 1):
            left = LAST_GROUP[J] - g + 1
            while len(coming) >= left:
                steps.append(coming.pop(0))
            if early is not None and early < M1 and g % 2 == 0:
                steps.append(("early", early))
                early += 1
            steps.append(("tiles", g))
            sums(g - SEL_LAG, False)
            sums(g - XSLOTS + 1, True)
        if J == 0:
            steps += turn(2)[1:]
        elif J == 1:
            steps += [("w", 2), ("w", 3)]
    sums(NGROUP - 1, True)
    while early < M1:
        steps.append(("early", early))
        early += 1
    return steps


PLAN = plan()
SPLITS = [s[1:] for s in PLAN if s[0] == "split"]


def pair_of(a, b):
    i, j = min(a, b), max(a, b)
    return i * (2 * F - i - 1) // 2 + (j - i - 1)


def lay_out_weights(w, W_top1):
    wst = np.zeros((NWCOL, G, K, WCHUNK, G, K), w.dtype)
    w1 = np.zeros((NZ * P, H1), W_top1.dtype)
    n = 0
    for g, (J, I0, nI, tiles) in enumerate(GROUPS):
        for i, tile in enumerate(tiles):
            I = I0 + i if nI > 1 else I0
            t = TILE_BASE[g] + i
            for src, rows in tile:
                c, at = n // WCHUNK, n % WCHUNK
                for r in rows:
                    a, b = ORDER[src], ORDER[G * I + r]
                    block = w[:, pair_of(a, b), :]
                    wst[c // G, c % G, :, at, r, :] = block if a > b else block.T
                    z = (t // ZTILES) * P + (t % G) * K + (t % ZTILES // G) * G + r
                    w1[z] = W_top1[pair_of(a, b)]
                n += 1
    return wst.reshape(NWCOL, P, WCOLS), w1


def dlrm_tower(nc, tables, ids, hot_ids, dense_t, wst, w1, w1d, w2, columns, y):
    with ExitStack() as ctx:
        def sb(name, shape, dt=F32):
            return ctx.enter_context(nc.sbuf_tensor(name, shape, dt))

        def sem(name):
            return ctx.enter_context(nc.semaphore(name))

        ids_sb = sb("ids_sb", [P, NCHUNK * F], I32)
        ident = sb("ident", [P, P])
        sel = sb("sel", [P, ZM, K])
        gathered = sb("gathered", [P, 2, NCHUNK, P])
        eT = sb("eT", [P, NBLK, B])
        halves = sb("halves", [P, NCHUNK * G, 4, K])
        stack = sb("stack", [P, 2, G, B])
        w_lo = sb("w_lo", [P, NWCOL, WCOLS])
        w_hi = sb("w_hi", [P, NWCOL, WCOLS])
        wring = sb("wring", [P, WSLOTS, WCHUNK, P])
        prod = sb("prod", [P, XSLOTS, GROUP, B])
        hot = sb("hot", [P, HOT_BUFS, G, B], BF16)
        slice_rows = sb("slice_rows", [P, NSLICE])
        slice_rows_int = sb("slice_rows_int", [P, NSLICE], I32)
        columns_sb = sb("columns_sb", [P, M1 + 2 * M2])
        b1_sb = columns_sb[:, 0:M1]
        b2_sb = columns_sb[:, M1:M1 + M2]
        w3_sb = columns_sb[:, M1 + M2:]
        y_sb = sb("y_sb", [1, B])
        room = sb("room", [P, (NZ + M1) * B])
        z_sb = room[:, 0:NZ * B].rearrange("p (k b) -> p k b", k=NZ)
        h_early = room[:, NZ * B:].rearrange("p (k b) -> p k b", k=M1)
        ntab = NSLICE * K
        part_cols = G * NHOT * ntab // 2
        parts = [room[:, part_cols * i:part_cols * i + part_cols].bitcast(BF16)
                 .rearrange("p (f c) -> p f c", f=G * NHOT) for i in range(3)]
        mlp = sb("mlp", [P, NZ * H1 + M1 * H2 + H1 + B])
        w1_sb = mlp[:, 0:NZ * H1].rearrange("p (k n) -> p k n", k=NZ)
        at = NZ * H1
        w2_sb = mlp[:, at:at + M1 * H2].rearrange("p (k n) -> p k n", k=M1)
        at += M1 * H2
        w1d_sb = mlp[0:NDENSE, at:at + H1]
        dense_sb = mlp[0:NDENSE, at + H1:at + H1 + B]
        tab = mlp[:, 0:G * NHOT * ntab].rearrange("p (f c) -> p f c", f=G * NHOT)
        ids_half = [mlp[:, NZ * H1 + G * B // 2 * i:NZ * H1 + G * B // 2 * (i + 1)].bitcast(F16)
                    .rearrange("p (f b) -> p f b", f=G) for i in range(2)]
        ids_wide = [eT[:, NBLK - G * (i + 1):NBLK - G * i, :].bitcast(I32) for i in range(2)]
        h1_sum = [prod[:, 0, m, :] if m < GROUP else prod[:, 1, 0, :] for m in range(M1)]
        h1_sb = [prod[:, 2, m, :] if m < GROUP else prod[:, 1, 1, :] for m in range(M1)]
        h2_sb = [prod[:, 3, m, :] for m in range(M2)]

        t_ps = [ctx.enter_context(nc.psum_tensor(f"t_ps{i}", [P, GROUP, B], F32)) for i in range(2)]
        z_ps = ctx.enter_context(nc.psum_tensor("z_ps", [P, B], F32))
        side_ps = ctx.enter_context(nc.psum_tensor("side_ps", [P, B], F32))
        h1_ps = [t_ps[0][:, 0, :], t_ps[0][:, 1, :], t_ps[0][:, 2, :], t_ps[1][:, 0, :]]
        h2_ps = [t_ps[1][:, 1, :], t_ps[1][:, 2, :]]
        y_ps = side_ps[0:1, :]

        look_ps = [t_ps[1][:, J, :] for J in range(NHOT)]

        def lift_ps(J, r):
            if J >= NHOT or r == 0:
                return side_ps[:, :]
            if r == 1:
                return z_ps[:, :]
            return t_ps[J // 2][:, r - 2, :]

        ids_in = sem("ids_in")
        ids_wide_in = [sem(f"ids_wide_in{J}") for J in range(NHOT)]
        tab_in = [sem(f"tab_in{J}") for J in range(NHOT)]
        w_in = [sem(f"w_in{c}") for c in range(NWCOL)]
        mlp_in = sem("mlp_in")
        consts_zero = sem("consts_zero")
        consts_made = sem("consts_made")
        pad_zeroed = sem("pad_zeroed")
        rows_numbered = sem("rows_numbered")
        rows_made = sem("rows_made")
        ids_half_made = sem("ids_half_made")
        part_made = sem("part_made")
        rest_made = sem("rest_made")
        hot_made = sem("hot_made")
        hot_used = sem("hot_used")
        rows_in = [sem(f"rows_in{J}") for J in range(NBLK)]
        turned = sem("turned")
        turned_back = sem("turned_back")
        eT_made = sem("eT_made")
        hi_made = sem("hi_made")
        lo_made = sem("lo_made")
        lo_copied = sem("lo_copied")
        lifted = sem("lifted")
        stack_made = sem("stack_made")
        w_hi_made = sem("w_hi_made")
        w_lo_made = sem("w_lo_made")
        wring_in = [sem(f"wring_in{i}") for i in range(WSLOTS)]
        tiles_made = sem("tiles_made")
        multiplied = sem("multiplied")
        summed = sem("summed")
        z_kept = sem("z_kept")
        early_made = sem("early_made")
        early_kept = sem("early_kept")
        h1_made = sem("h1_made")
        h1_added = sem("h1_added")
        h1_kept = sem("h1_kept")
        h2_made = sem("h2_made")
        h2_kept = sem("h2_kept")
        y_made = sem("y_made")
        y_kept = sem("y_kept")
        y_out = sem("y_out")

        mlp_loads = [(w1_sb, w1.rearrange("(k p) n -> p k n", p=P)),
                     (w2_sb, w2.rearrange("(k p) n -> p k n", p=P)),
                     (w1d_sb, w1d), (dense_sb, dense_t), (columns_sb[:, :], columns)]
        sums = [s for s in PLAN if s[0] == "sums"]
        sums_through = [next(i + 1 for i, s in enumerate(sums) if s[1] + s[2] >= TILE_BASE[g + 1])
                        for g in range(NGROUP)]
        chunk_last_group = [next(g for g in range(NGROUP)
                                 if PASS_BASE[g + 1] >= min(NPASS, (c + 1) * WCHUNK))
                            for c in range(NWCHUNK)]

        block = ctx.enter_context(nc.Block())

        @block.sync
        def _(sp):
            def load_hot(J):
                for f in range(G * J, G * J + G):
                    sp.dma_start(tab[0:HP, f, :], tables[ORDER[f]].rearrange("(p c) d -> p (c d)", c=NSLICE))\
                        .then_inc(tab_in[J], 16)
                sp.dma_start(ids_wide[J % 2], hot_ids[J:J + 1, :, :].broadcast_to([P, G, B]))\
                    .then_inc(ids_wide_in[J], 16)

            def load_w(c):
                sp.dma_start(w_lo[:, c, :], wst[c, :, :]).then_inc(w_in[c], 16)

            def fill_ring(c):
                sp.wait_ge(w_hi_made, c // G + 1)
                sp.wait_ge(w_lo_made, c // G + 1)
                if c >= WSLOTS:
                    sp.wait_ge(tiles_made, chunk_last_group[c - WSLOTS] + 1)
                q = K * (c % G)
                for i, part in enumerate((w_hi, w_lo, w_hi, w_lo)):
                    sp.dma_start(wring[K * i:K * i + K, c % WSLOTS, :, :].rearrange("p a b -> p (a b)"),
                                 part[q:q + K, c // G, :]).then_inc(wring_in[c % WSLOTS], 16)

            sp.dma_start(ids_sb[:, :], ids).then_inc(ids_in, 16)
            load_hot(0)
            load_hot(1)
            load_w(0)
            sp.wait_ge(ids_half_made, 1)
            load_hot(2)
            for c in range(1, NWCOL):
                load_w(c)
            fill_ring(0)
            fill_ring(1)
            sp.wait_ge(rest_made, 2 * NHOT)
            sp.wait_ge(part_made, 2 * NHOT)
            sp.wait_ge(hot_made, NHOT * NSLICE)
            for dst, src in mlp_loads:
                sp.dma_start(dst, src).then_inc(mlp_in, 16)
            for c in range(WSLOTS, NWCHUNK):
                fill_ring(c)
            sp.wait_ge(y_kept, 1)
            sp.dma_start(y.rearrange("b o -> o b"), y_sb[:, :]).then_inc(y_out, 16)
            sp.wait_ge(y_out, 16)

        @block.gpsimd
        def _(pool):
            pool.memset(ident[:, :], 0.0).then_inc(consts_zero, 1)
            pool.memset(sel[:, :, :], 1.0).then_inc(consts_zero, 1)
            pool.iota(slice_rows_int[:, :], pattern=[[1, NSLICE]], base=0,
                      channel_multiplier=NSLICE).then_inc(rows_numbered, 1)
            pool.wait_ge(consts_zero, 2)
            pool.affine_select(out=ident[:, :], in_=ident[:, :], compare_op=ALU.not_equal, fill=1.0, base=0,
                               pattern=[[-1, P]], channel_multiplier=1).then_inc(consts_made, 1)
            pool.affine_select(out=sel[:, :, :], in_=sel[:, :, :], compare_op=ALU.is_ge, fill=0.0, base=0,
                               pattern=[[P, ZM], [-K, K]], channel_multiplier=1).then_inc(consts_made, 1)
            pool.wait_ge(consts_made, 2)
            pool.affine_select(out=sel[:, :, :], in_=sel[:, :, :], compare_op=ALU.is_ge, fill=0.0, base=K - 1,
                               pattern=[[-P, ZM], [K, K]], channel_multiplier=-1).then_inc(consts_made, 1)
            pool.wait_ge(ids_in, 16)
            for J in range(NHOT, NBLK):
                if J >= NHOT + 2:
                    pool.wait_ge(turned, J - 2 - NHOT + 1)
                    pool.wait_ge(lo_made, J - 2 + 1)
                for r in range(in_block(J)):
                    f = ORDER[G * J + r]
                    for b in range(NCHUNK):
                        pool.indirect_dma_start(
                            gathered[:, J % 2, b, K * r:K * r + K], None, tables[f],
                            bass.IndirectOffsetOnAxis(ap=ids_sb[:, F * b + f:F * b + f + 1], axis=0),
                        ).then_inc(rows_in[J], 16)

        @block.scalar
        def _(act):
            act.wait_ge(rows_numbered, 1)
            act.activation(slice_rows[:, :], slice_rows_int[:, :], ACT.Copy).then_inc(rows_made, 1)
            looked_up = 0
            for step in PLAN:
                if step[0] == "w":
                    c = step[1]
                    act.wait_ge(w_in[c], 16)
                    act.activation(w_hi[:, c, :].bitcast(F32R), w_lo[:, c, :], ACT.Copy).then_inc(w_hi_made, 1)
                elif step[0] == "ids":
                    J = step[1]
                    act.wait_ge(ids_wide_in[J], 16)
                    if J >= 2:
                        act.wait_ge(hot_made, NSLICE * (J - 1))
                    act.activation(ids_half[J % 2], ids_wide[J % 2], ACT.Copy).then_inc(ids_half_made, 1)
                elif step[0] == "split":
                    J, i = step[1:]
                    of = slice(G * J, G * J + G)
                    if i == 0:
                        act.wait_ge(tab_in[J], 16 * G)
                    else:
                        act.wait_ge(rest_made, SPLITS.index((J, 0)) + 1)
                    act.activation(parts[i][0:HP, of, :], tab[0:HP, of, :], ACT.Copy).then_inc(part_made, 1)
                elif step[0] == "keep":
                    J = step[1]
                    n = K * in_block(J)
                    if J < NHOT:
                        act.wait_ge(hot_used, NSLICE * (J + 1))
                        if J == 0:
                            act.wait_ge(ids_half_made, 2)
                        act.activation(eT[:, J, :], look_ps[J], ACT.Copy).then_inc(eT_made, 1)
                    else:
                        act.wait_ge(turned, J - NHOT + 1)
                        act.activation(eT[0:n, J, :], side_ps[0:n, :], ACT.Copy).then_inc(eT_made, 1)
                elif step[0] == "halve":
                    J = step[1]
                    n = in_block(J)
                    if J > 0:
                        act.wait_ge(lifted, G * J)
                    if J < NHOT:
                        act.wait_ge(turned_back, J + 1)
                        src = side_ps[:, :].rearrange("p (s o k) -> p s o k", o=1, k=K)
                        act.activation(halves[:, :, 0:2, :].bitcast(F32R),
                                       src.broadcast_to([P, NCHUNK * G, 2, K]), ACT.Copy).then_inc(hi_made, 1)
                    else:
                        act.wait_ge(rows_in[J], 16 * n * NCHUNK)
                        if n < G:
                            for b in range(NCHUNK):
                                src = gathered[:, J % 2, b, 0:K * n].rearrange("p (r o k) -> p r o k", o=1, k=K)
                                mm = act.activation(halves[:, G * b:G * b + n, 0:2, :].bitcast(F32R),
                                                    src.broadcast_to([P, n, 2, K]), ACT.Copy)
                            mm.then_inc(hi_made, 1)
                        else:
                            src = gathered[:, J % 2, :, :].rearrange("p s (r o k) -> p (s r) o k", o=1, k=K)
                            act.activation(halves[:, :, 0:2, :].bitcast(F32R),
                                           src.broadcast_to([P, NCHUNK * G, 2, K]), ACT.Copy).then_inc(hi_made, 1)
                    act.wait_ge(lo_made, J + 1)
                    if n < G:
                        for b in range(NCHUNK):
                            ins = act.activation(halves[:, G * b:G * b + n, 3, :].bitcast(F32R),
                                                 halves[:, G * b:G * b + n, 2, :], ACT.Copy)
                        ins.then_inc(lo_copied, 1)
                    else:
                        act.activation(halves[:, :, 3, :].bitcast(F32R), halves[:, :, 2, :],
                                       ACT.Copy).then_inc(lo_copied, 1)
                elif step[0] == "lift":
                    J, r = step[1:]
                    act.wait_ge(lifted, G * J + r + 1)
                    if J >= 2 and r == 0:
                        act.wait_ge(tiles_made, LAST_GROUP[J - 2] + 1)
                    act.activation(stack[:, J % 2, r, :].bitcast(F32R), lift_ps(J, r),
                                   ACT.Copy).then_inc(stack_made, 1)
                elif step[0] == "z":
                    act.wait_ge(summed, step[2])
                    act.activation(z_sb[:, step[1], :], z_ps[:, :], ACT.Copy).then_inc(z_kept, 1)
                elif step[0] == "early":
                    m = step[1]
                    if m == 0:
                        act.wait_ge(mlp_in, 16 * len(mlp_loads))
                    act.wait_ge(early_made, m + 1)
                    act.activation(h_early[:, m, :], side_ps[:, :], ACT.Identity,
                                   bias=b1_sb[:, m:m + 1]).then_inc(early_kept, 1)
            for m in range(M1):
                act.wait_ge(h1_added, m + 1)
                act.activation(h1_sb[m], h1_sum[m], ACT.Relu).then_inc(h1_kept, 1)
            for m in range(M2):
                act.wait_ge(h2_made, m + 1)
                act.activation(h2_sb[m], h2_ps[m], ACT.Relu, bias=b2_sb[:, m:m + 1]).then_inc(h2_kept, 1)
            act.wait_ge(y_made, 1)
            act.activation(y_sb[:, :], y_ps, ACT.Copy).then_inc(y_kept, 1)

        @block.vector
        def _(dve):
            for step in PLAN:
                if step[0] == "w":
                    c = step[1]
                    dve.wait_ge(w_hi_made, c + 1)
                    dve.tensor_tensor(w_lo[:, c, :].bitcast(F32R), w_lo[:, c, :], w_hi[:, c, :],
                                      ALU.subtract).then_inc(w_lo_made, 1)
                elif step[0] == "split":
                    J, i = step[1:]
                    of = slice(G * J, G * J + G)
                    dve.wait_ge(part_made, SPLITS.index((J, i)) + 1)
                    if i == 1:
                        dve.wait_ge(rest_made, SPLITS.index((J, 0)) + 1)
                    rest = tab[0:HP, of, :]
                    dve.tensor_tensor(parts[2][0:HP, of, :] if i else rest, rest, parts[i][0:HP, of, :],
                                      ALU.subtract).then_inc(rest_made, 1)
                elif step[0] == "look":
                    J, c0, c1 = step[1:]
                    if c0 == 0:
                        dve.wait_ge(rows_made, 1)
                        dve.wait_ge(ids_half_made, J + 1)
                    for c in range(c0, c1):
                        n = NSLICE * J + c
                        if n >= HOT_BUFS:
                            dve.wait_ge(hot_used, n - HOT_BUFS + 1)
                        dve.tensor_scalar(hot[0:HP, n % HOT_BUFS, :, :], ids_half[J % 2][0:HP, :, :],
                                          slice_rows[0:HP, c:c + 1], None, ALU.is_equal).then_inc(hot_made, 1)
                elif step[0] == "keep" and step[1] == NBLK - 1:
                    dve.memset(eT[K * in_block(NBLK - 1):P, NBLK - 1, :], 0.0).then_inc(pad_zeroed, 1)
                    dve.wait_ge(pad_zeroed, 1)
                elif step[0] == "halve":
                    J = step[1]
                    n = in_block(J)
                    dve.wait_ge(hi_made, J + 1)
                    if J < NHOT:
                        dve.tensor_tensor(halves[:, :, 2, :].bitcast(F32R),
                                          side_ps[:, :].rearrange("p (s k) -> p s k", k=K),
                                          halves[:, :, 0, :], ALU.subtract).then_inc(lo_made, 1)
                    else:
                        src = gathered[:, J % 2, :, 0:K * n].rearrange("p s (r k) -> p s r k", k=K)
                        by_chunk = halves[:, :, :, :].rearrange("p (s r) i k -> p s r i k", r=G)
                        dve.tensor_tensor(by_chunk[:, :, 0:n, 2, :].bitcast(F32R), src,
                                          by_chunk[:, :, 0:n, 0, :], ALU.subtract).then_inc(lo_made, 1)
                elif step[0] == "tiles":
                    g = step[1]
                    J, I0, nI, tiles = GROUPS[g]
                    n = len(tiles)
                    dve.wait_ge(tiles_made, g + 1)
                    if g == FIRST_GROUP[J]:
                        dve.wait_ge(eT_made, J + 1)
                    if g >= XSLOTS:
                        dve.wait_ge(summed, sums_through[g - XSLOTS])
                    if nI > 1:
                        field = eT[:, I0:I0 + n, :]
                    else:
                        field = eT[:, I0:I0 + 1, :].broadcast_to([P, n, B])
                    dve.tensor_tensor(prod[:, g % XSLOTS, 0:n, :], t_ps[g % 2][:, 0:n, :], field,
                                      ALU.mult).then_inc(multiplied, 1)
            for m in range(M1):
                dve.wait_ge(h1_made, m + 1)
                dve.wait_ge(early_kept, m + 1)
                if m == 0:
                    dve.wait_ge(summed, len(sums))
                dve.tensor_tensor(h1_sum[m], h1_ps[m], h_early[:, m, :], ALU.add).then_inc(h1_added, 1)

        @block.tensor
        def _(pe):
            passes = 0
            side_used = []

            def side_free():
                if side_used:
                    pe.wait_ge(*side_used[-1])

            def lift_bank_free(J, r):
                if J < NHOT and r > 0:
                    if J > 0:
                        pe.wait_ge(stack_made, G * (J - 1) + r + 1)
                else:
                    side_free()

            for step in PLAN:
                if step[0] == "look":
                    J, c0, c1 = step[1:]
                    if c0 == 0:
                        pe.wait_ge(rest_made, SPLITS.index((J, 1)) + 1)
                    for c in range(c0, c1):
                        n = NSLICE * J + c
                        pe.wait_ge(hot_made, n + 1)
                        for i in range(3):
                            for r in range(G):
                                mm = pe.matmul(look_ps[J][K * r:K * r + K, :],
                                               parts[i][0:HP, G * J + r, K * c:K * c + K],
                                               hot[0:HP, n % HOT_BUFS, r, :],
                                               start=(c == 0 and i == 0), stop=(c == NSLICE - 1 and i == 2))
                        mm.then_inc(hot_used, 1)
                elif step[0] == "keep" and step[1] >= NHOT:
                    J = step[1]
                    n = K * in_block(J)
                    pe.wait_ge(rows_in[J], 16 * in_block(J) * NCHUNK)
                    side_free()
                    for b in range(NCHUNK):
                        mm = pe.transpose(side_ps[0:n, P * b:P * b + P], gathered[:, J % 2, b, 0:n], ident[:, :])
                    mm.then_inc(turned, 1)
                    side_used.append((eT_made, J + 1))
                elif step[0] == "halve" and step[1] < NHOT:
                    J = step[1]
                    pe.wait_ge(consts_made, 3)
                    pe.wait_ge(eT_made, J + 1)
                    side_free()
                    for b in range(NCHUNK):
                        mm = pe.transpose(side_ps[:, P * b:P * b + P], eT[:, J, P * b:P * b + P], ident[:, :])
                    mm.then_inc(turned_back, 1)
                    side_used.append((lo_made, J + 1))
                elif step[0] == "lift":
                    J, r = step[1:]
                    pe.wait_ge(lo_copied, J + 1)
                    lift_bank_free(J, r)
                    for b in range(NCHUNK):
                        mm = pe.transpose(lift_ps(J, r)[:, P * b:P * b + P],
                                          halves[:, G * b + r, :, :].rearrange("p i k -> p (i k)"), ident[:, :])
                    mm.then_inc(lifted, 1)
                    if J >= NHOT or r == 0:
                        side_used.append((stack_made, G * J + r + 1))
                elif step[0] == "tiles":
                    g = step[1]
                    J, I0, nI, tiles = GROUPS[g]
                    if g == FIRST_GROUP[J]:
                        pe.wait_ge(stack_made, G * J + in_block(J))
                    if g == 0:
                        pe.wait_ge(stack_made, 2 * G)
                    if g == 1:
                        pe.wait_ge(stack_made, 3 * G)
                        pe.wait_ge(eT_made, NHOT)
                    if g >= 2:
                        pe.wait_ge(multiplied, g - 1)
                    for i, tile in enumerate(tiles):
                        for k, (src, _) in enumerate(tile):
                            c = passes // WCHUNK
                            if passes % WCHUNK == 0:
                                pe.wait_ge(wring_in[c % WSLOTS], 16 * G * (c // WSLOTS + 1))
                            mm = pe.matmul(t_ps[g % 2][:, i, :],
                                           wring[:, c % WSLOTS, passes % WCHUNK, :].bitcast(F32R),
                                           stack[:, J % 2, src - G * J, :].bitcast(F32R),
                                           start=(k == 0), stop=(k == len(tile) - 1))
                            passes += 1
                    mm.then_inc(tiles_made, 1)
                elif step[0] == "sums":
                    for t in range(step[1], step[1] + step[2]):
                        g = GROUP_OF_TILE[t]
                        u = t % ZTILES
                        if t == step[1] or g != GROUP_OF_TILE[t - 1]:
                            pe.wait_ge(multiplied, g + 1)
                        if u == 0 and t > 0:
                            pe.wait_ge(z_kept, t // ZTILES)
                        mm = pe.matmul(z_ps[K * (u % G):K * (u % G) + K, :], sel[:, u // G, :],
                                       prod[:, g % XSLOTS, t - TILE_BASE[g], :],
                                       start=(u < G), stop=(u >= ZTILES - G or t >= NTILE - G))
                    mm.then_inc(summed, 1)
                elif step[0] == "early":
                    m = step[1]
                    if m == 0:
                        pe.wait_ge(mlp_in, 16 * len(mlp_loads))
                        pe.wait_ge(z_kept, EARLY_Z)
                    side_free()
                    cols = slice(P * m, P * m + P)
                    pe.matmul(side_ps[:, :], w1d_sb[:, cols], dense_sb[:, :], start=True, stop=False)
                    for zb in range(EARLY_Z):
                        mm = pe.matmul(side_ps[:, :], w1_sb[:, zb, cols], z_sb[:, zb, :],
                                       start=False, stop=(zb == EARLY_Z - 1))
                    mm.then_inc(early_made, 1)
                    side_used.append((early_kept, m + 1))
            pe.wait_ge(multiplied, NGROUP)
            for m in range(M1):
                for zb in range(EARLY_Z, NZ):
                    pe.wait_ge(z_kept, zb + 1)
                    mm = pe.matmul(h1_ps[m], w1_sb[:, zb, P * m:P * m + P], z_sb[:, zb, :],
                                   start=(zb == EARLY_Z), stop=(zb == NZ - 1))
                mm.then_inc(h1_made, 1)
            for k in range(M1):
                pe.wait_ge(h1_kept, k + 1)
                for m in range(M2):
                    mm = pe.matmul(h2_ps[m], w2_sb[:, k, P * m:P * m + P], h1_sb[k],
                                   start=(k == 0), stop=(k == M1 - 1))
                    if k == M1 - 1:
                        mm.then_inc(h2_made, 1)
            side_free()
            for k in range(M2):
                pe.wait_ge(h2_kept, k + 1)
                mm = pe.matmul(y_ps, w3_sb[:, k:k + 1], h2_sb[k], start=(k == 0), stop=(k == M2 - 1))
            mm.then_inc(y_made, 1)


def kernel(**inputs):
    import concourse.bacc as bacc
    from concourse.bass_utils import run_bass_kernel_spmd

    a = {k: np.asarray(v) for k, v in inputs.items()}
    wst, w1 = lay_out_weights(a["L0_rec_w"], a["W_top1"])
    arrays = {f"tbl_{f}": np.ascontiguousarray(a[f"tbl_{f}"]) for f in range(F)}
    arrays["ids"] = np.ascontiguousarray(a["ids"].reshape(NCHUNK, P, F).transpose(1, 0, 2).reshape(P, -1))
    arrays["hot_ids"] = np.ascontiguousarray(a["ids"].T[HOT_FIELDS].reshape(NHOT, G, B))
    arrays["dense_t"] = np.ascontiguousarray(a["dense_ctx"].T)
    arrays["wst"], arrays["w1"] = wst, w1
    arrays["w1d"] = np.ascontiguousarray(a["W_top1"][F * (F - 1) // 2:])
    arrays["w2"] = np.ascontiguousarray(a["W_top2"])
    arrays["columns"] = np.concatenate(
        [a[n].reshape(-1, P).T for n in ("b_top1", "b_top2", "W_top3")], axis=1)

    nc = bacc.Bacc("TRN2", target_bir_lowering=False, num_devices=1)
    ap = {name: nc.dram_tensor(name, v.shape, mybir.dt.from_np(v.dtype), kind="ExternalInput").ap()
          for name, v in arrays.items()}
    y = nc.dram_tensor("y", (B, 1), F32, kind="ExternalOutput").ap()
    dlrm_tower(nc, [ap[f"tbl_{f}"] for f in range(F)],
               *(ap[n] for n in ("ids", "hot_ids", "dense_t", "wst", "w1", "w1d", "w2", "columns")), y)
    r = run_bass_kernel_spmd(nc, [arrays], core_ids=[0])
    return r.results[0]["y"]
```

```python
from contextlib import ExitStack

import numpy as np

import concourse.bass as bass
from concourse import mybir

ALU = mybir.AluOpType
ACT = mybir.ActivationFunctionType
BF16 = mybir.dt.bfloat16
F16 = mybir.dt.float16
F32 = mybir.dt.float32
F32R = mybir.dt.float32r
I32 = mybir.dt.int32

P = 128
F = 39
K = 32
B = 512
NCHUNK = B // P
G = P // K
NBLK = -(-F // G)
NDENSE = 16
H1, H2 = 512, 256
M1, M2 = H1 // P, H2 // P

TABLE_ROWS = [12500, 125000, 1000, 12500, 12500, 125000, 1000, 1250, 125000, 1000, 1250, 125000, 12500,
              125000, 12500, 1000, 1250, 125000, 1000, 12500, 1250, 12500, 1250, 1000, 1000, 1000, 12500,
              1000, 12500, 12500, 1000, 1000, 12500, 1250, 1250, 12500, 12500, 1000, 12500]
HOT_BLOCKS = [0, 1, 3]
GATHERED = [J for J in range(NBLK) if J not in HOT_BLOCKS]
NHOT = len(HOT_BLOCKS)
HOT_ROWS = 1000
NSLICE = 8
HP = HOT_ROWS // NSLICE
HOT_BUFS = 4
GATHER_BUFS = 3
STACKS = 3
HOT_FIELDS = [f for f in range(F) if TABLE_ROWS[f] == HOT_ROWS][:G * NHOT]
ORDER = [f for f in range(F) if f not in HOT_FIELDS]
for _h, _J in enumerate(HOT_BLOCKS):
    ORDER[G * _J:G * _J] = HOT_FIELDS[G * _h:G * _h + G]

GROUP = 3
XSLOTS = 4
WCHUNK = 14
WSLOTS = 2
ZTILES = P // G
ZM = ZTILES // G


def in_block(J):
    return min(G, F - G * J)


def make_schedule():
    groups = []
    for J in range(NBLK):
        n = in_block(J)
        src = [G * J + r for r in range(n)]
        every = list(range(G))
        whole = J - J % GROUP
        for s in src:
            for I0 in range(0, whole, GROUP):
                groups.append((J, I0, GROUP, [[(s, every)]] * GROUP))
        for I in range(whole, J):
            groups.append((J, I, 1, [[(s, every)] for s in src[:GROUP]]))
        if n > GROUP and J > whole:
            groups.append((J, whole, J - whole, [[(src[GROUP], every)]] * (J - whole)))
        s = src
        if n == 4:
            groups.append((J, J, 1, [[(s[2], [0]), (s[0], [1]), (s[1], [2, 3])], [(s[3], [0, 2])]]))
        else:
            groups.append((J, J, 1, [[(s[2], [0]), (s[0], [1]), (s[1], [2])]]))
    return groups


GROUPS = make_schedule()
NGROUP = len(GROUPS)
TILE_BASE = [0]
PASS_BASE = [0]
for _g in GROUPS:
    TILE_BASE.append(TILE_BASE[-1] + len(_g[3]))
    PASS_BASE.append(PASS_BASE[-1] + sum(len(t) for t in _g[3]))
NTILE, NPASS = TILE_BASE[-1], PASS_BASE[-1]
NZ = -(-NTILE // ZTILES)
NWCHUNK = -(-NPASS // WCHUNK)
WCOLS = WCHUNK * P
NWCOL = -(-NWCHUNK // G)
GROUP_OF_TILE = [g for g in range(NGROUP) for _ in GROUPS[g][3]]
LAST_GROUP = [max(g for g in range(NGROUP) if GROUPS[g][0] == J) for J in range(NBLK)]
FIRST_GROUP = [min(g for g in range(NGROUP) if GROUPS[g][0] == J) for J in range(NBLK)]
ROUNDS = [[0], [1], [2], [3]]
EARLY_Z = sum(len(blocks) for blocks in ROUNDS)
PACE = 3
Z_LAG = 3
TURN_LEADS = {4: 8, 5: 7, 6: 6, 7: 6, 8: 6, 9: 6}
POOL_WORK = {
    (2, 3): ("rest", 1, 1), (4, 0): ("rest", 2, 1), (8, 0): ("w_lo", 2), (8, 3): ("w_lo", 3)}
SEL_LAG = 2


def plan():
    steps, done = [], 0
    early = [(m, n, i) for n in range(len(ROUNDS)) for m in range(M1) for i in range(len(ROUNDS[n]))]
    long, since = EARLY_Z, 0

    def there(zb):
        names = [step[:2] for step in steps]
        return ("z", zb) in names and sum(n[0] == "tiles" for n in names[names.index(("z", zb)):]) > Z_LAG

    def sums(upto, exact):
        nonlocal done
        end = TILE_BASE[upto + 1] if upto >= 0 else 0
        while done < end and (exact or end - done >= G - done % G):
            n = min(G - done % G, end - done)
            steps.append(("sums", done, n))
            done += n
            if done % ZTILES == 0 or done == NTILE:
                steps.append(("z", (done - 1) // ZTILES, sum(s[0] == "sums" for s in steps)))

    steps += [("rest", 2, 1), ("rest", 0, 0), ("rest", 0, 1), ("look", 0, 0, 1), ("split", 0, 0),
              ("split", 0, 1), ("ids", 0), ("look", 0, 1, 2), ("rest", 1, 0), ("split", 1, 0), ("w_hi", 0),
              ("look", 0, 2, 3), ("ids", 1), ("look", 0, 3, 6), ("split", 1, 1), ("split", 2, 0),
              ("look", 0, 6, 8), ("keep", 0), ("rest", 2, 0), ("look", 1, 0, 1), ("halve", 0), ("stack", 0),
              ("look", 1, 1, 2), ("split", 2, 1), ("look", 1, 2, 4), ("w_lo", 0), ("rest", 1, 1), ("ids", 2),
              ("keep", 2), ("look", 1, 4, 7), ("halve", 2), ("look", 1, 7, 8), ("look", 2, 0, 1), ("stack", 2),
              ("look", 2, 1, 2), ("keep", 1), ("look", 2, 2, 6), ("halve", 1), ("look", 2, 6, 8), ("stack", 1),
              ("keep", 3), ("tiles", 0)]
    keep_at = {J: LAST_GROUP[J - 1] + 1 - lead for J, lead in TURN_LEADS.items()}
    for J in range(1, NBLK):
        for g in range(FIRST_GROUP[J], LAST_GROUP[J] + 1):
            if g in (1, 2):
                steps.append((("halve", "stack")[g - 1], 3))
            steps += [(part, T) for T in keep_at for i, part in enumerate(("keep", "halve", "stack"))
                      if g == keep_at[T] + i]
            steps.append(("tiles", g))
            until_keep = min((at - g for at in keep_at.values() if at > g), default=NGROUP)
            since += 1
            if early and there(ROUNDS[early[0][1]][-1]) and since >= PACE and (
                    early[0][2] > 0 or until_keep > PACE * (len(ROUNDS[early[0][1]]) - 1) + 1):
                steps.append(("early", *early.pop(0)))
                since = 0
            elif not early and J == NBLK - 1 and long < NZ - 1 and there(long) and since >= PACE:
                steps.append(("long", long))
                long += 1
                since = 0
            sums(g - SEL_LAG, False)
            sums(g - XSLOTS + 1, True)
        steps += [(part, c) for c in {1: [1], 3: [2, 3]}.get(J, []) for part in ("w_hi", "w_lo")]
    sums(NGROUP - 2, True)
    steps += [("early", *e) for e in early]
    steps += [("long", k) for k in range(long, NZ - 1)]
    late = [("late", m, zb) for m in range(M1 - 1) for zb in range(EARLY_Z, NZ - 1)]
    steps += late[:-1]
    sums(NGROUP - 1, True)
    steps += late[-1:]
    return [step for step in steps if step not in POOL_WORK.values()]


PLAN = plan()
LAST_FIRST = [M1 - 1] + list(range(M1 - 1))
assert NGROUP % 2 == 0
SPLITS = [s[1:] for s in PLAN if s[0] == "split"]
TURNS = [s[1] for s in PLAN if s[0] == "keep"]
assert all([s[1] for s in PLAN if s[0] == part] == TURNS for part in ("halve", "stack"))


def turns(J):
    return TURNS.index(J) + 1


def pair_of(a, b):
    i, j = min(a, b), max(a, b)
    return i * (2 * F - i - 1) // 2 + (j - i - 1)


def z_row(t, r):
    return (t // ZTILES) * P + (t % G) * K + (t % ZTILES // G) * G + r


_taken = {(TILE_BASE[g] + i, r) for g in range(NGROUP) for i, tile in enumerate(GROUPS[g][3])
          for _, rows in tile for r in rows}
_free = [[z_row(t, r) for r in range(G) if (t, r) not in _taken] for t in range(NTILE)]
DENSE_ROWS = [(rows[0], rows[1] - rows[0]) for rows in _free if len(rows) == 2][:NDENSE // 2]
assert len(DENSE_ROWS) == NDENSE // 2
DENSE_BLOCKS = sorted({first // P for first, _ in DENSE_ROWS})


def lay_out_weights(w, W_top1):
    wst = np.zeros((NWCOL, G, K, WCHUNK, G, K), w.dtype)
    w1 = np.zeros((NZ * P, H1), W_top1.dtype)
    n = 0
    for g, (J, I0, nI, tiles) in enumerate(GROUPS):
        for i, tile in enumerate(tiles):
            I = I0 + i if nI > 1 else I0
            t = TILE_BASE[g] + i
            for src, rows in tile:
                c, at = n // WCHUNK, n % WCHUNK
                for r in rows:
                    a, b = ORDER[src], ORDER[G * I + r]
                    block = w[:, pair_of(a, b), :]
                    wst[c // G, c % G, :, at, r, :] = block if a > b else block.T
                    w1[z_row(t, r)] = W_top1[pair_of(a, b)]
                n += 1
    for i, (first, step) in enumerate(DENSE_ROWS):
        w1[first:first + step + 1:step] = W_top1[F * (F - 1) // 2 + 2 * i:][:2]
    return wst.reshape(NWCOL, P, WCOLS), w1


def dlrm_tower(nc, tables, ids, hot_ids, dense_t, wst, w1, w2, columns, y):
    with ExitStack() as ctx:
        def sb(name, shape, dt=F32):
            return ctx.enter_context(nc.sbuf_tensor(name, shape, dt))

        def sem(name):
            return ctx.enter_context(nc.semaphore(name))

        ids_sb = sb("ids_sb", [P, NCHUNK * F], I32)
        ident = sb("ident", [P, P])
        sel = sb("sel", [P, ZM, K])
        gathered = sb("gathered", [P, GATHER_BUFS, NCHUNK, P])
        eT = sb("eT", [P, NBLK, B])
        hi_lo = sb("hi_lo", [P, 2, 2, B])
        stack = sb("stack", [P, STACKS, G, B])
        w_lo = sb("w_lo", [P, NWCOL, WCOLS])
        w_hi = sb("w_hi", [P, NWCOL, WCOLS])
        wring = sb("wring", [P, WSLOTS, WCHUNK, P])
        prod = sb("prod", [P, XSLOTS, GROUP, B])
        slice_rows = sb("slice_rows", [P, NSLICE])
        slice_rows_int = sb("slice_rows_int", [P, NSLICE], I32)
        columns_sb = sb("columns_sb", [P, M1 + 2 * M2])
        b1_sb = columns_sb[:, 0:M1]
        b2_sb = columns_sb[:, M1:M1 + M2]
        w3_sb = columns_sb[:, M1 + M2:]
        y_sb = sb("y_sb", [1, B])
        room = sb("room", [P, (NZ + M1) * B])
        z_sb = room[:, 0:NZ * B].rearrange("p (k b) -> p k b", k=NZ)
        h_early = room[:, NZ * B:].rearrange("p (k b) -> p k b", k=M1)
        early_sum = [[h_early[:, m, :] for m in range(M1)]] + [
            [w_lo[:, n, B * m:B * m + B] if m < GROUP else w_hi[:, n, 0:B] for m in range(M1)]
            for n in range(len(ROUNDS) - 1)]
        ntab = NSLICE * K
        part_cols = G * NHOT * ntab // 2
        parts = [room[:, part_cols * i:part_cols * i + part_cols].bitcast(BF16)
                 .rearrange("p (f c) -> p f c", f=G * NHOT) for i in range(3)]
        mlp = sb("mlp", [P, NZ * H1 + max(M1 * H2, G * B)])
        w1_sb = mlp[:, 0:NZ * H1].rearrange("p (k n) -> p k n", k=NZ)
        at = NZ * H1
        w2_sb = mlp[:, at:at + M1 * H2].rearrange("p (k n) -> p k n", k=M1)
        tab = mlp[:, 0:G * NHOT * ntab].rearrange("p (f c) -> p f c", f=G * NHOT)
        ids_half = [mlp[:, NZ * H1 + G * B // 2 * i:NZ * H1 + G * B // 2 * (i + 1)].bitcast(F16)
                    .rearrange("p (f b) -> p f b", f=G) for i in range(2)]
        hot = [sb("hot", [P, G, B], BF16)] + [
            prod[:, slot, 0:G // 2, :].bitcast(BF16).rearrange("p a (c b) -> p (a c) b", b=B)
            for slot in range(1, XSLOTS)]
        ids_wide = [eT[:, NBLK - G * (i + 1):NBLK - G * i, :].bitcast(I32) for i in range(2)]
        h1_sum = [prod[:, 0, m, :] if m < GROUP else prod[:, 1, 0, :] for m in range(M1)]
        h1_sb = [prod[:, 2, m, :] if m < GROUP else prod[:, 1, 1, :] for m in range(M1)]
        h2_sb = [prod[:, 3, m, :] for m in range(M2)]

        t_ps = [ctx.enter_context(nc.psum_tensor(f"t_ps{i}", [P, GROUP, B], F32)) for i in range(2)]
        z_ps = ctx.enter_context(nc.psum_tensor("z_ps", [P, B], F32))
        side_ps = ctx.enter_context(nc.psum_tensor("side_ps", [P, B], F32))
        h1_ps = [t_ps[0][:, 0, :], t_ps[0][:, 1, :], t_ps[0][:, 2, :], side_ps[:, :]]
        h2_ps = [t_ps[1][:, 1, :], t_ps[1][:, 2, :]]
        y_ps = z_ps[0:1, :]

        look_ps = [t_ps[1][:, 0, :], t_ps[1][:, 1, :], z_ps[:, :]]

        ids_in = sem("ids_in")
        ids_wide_in = [sem(f"ids_wide_in{J}") for J in range(NHOT)]
        tab_in = [sem(f"tab_in{J}") for J in range(NHOT)]
        w_in = [sem(f"w_in{c}") for c in range(NWCOL)]
        mlp_in = sem("mlp_in")
        consts_zero = sem("consts_zero")
        consts_made = sem("consts_made")
        pad_zeroed = sem("pad_zeroed")
        rows_numbered = sem("rows_numbered")
        rows_made = sem("rows_made")
        ids_half_made = sem("ids_half_made")
        part_made = sem("part_made")
        rest_made = [sem(f"rest_made{h}") for h in range(NHOT)]
        hot_made = sem("hot_made")
        hot_used = sem("hot_used")
        rows_in = [sem(f"rows_in{J}") for J in range(NBLK)]
        turned = sem("turned")
        eT_made = sem("eT_made")
        hi_made = sem("hi_made")
        lo_made = sem("lo_made")
        stack_hi_made = sem("stack_hi_made")
        stack_lo_made = sem("stack_lo_made")
        stacked = [sem(f"stacked{i}") for i in range(STACKS)]
        w_hi_made = sem("w_hi_made")
        w_lo_made = [sem(f"w_lo_made{c}") for c in range(NWCOL)]
        wring_in = [sem(f"wring_in{i}") for i in range(WSLOTS)]
        tiles_made = sem("tiles_made")
        multiplied = sem("multiplied")
        summed = sem("summed")
        z_kept = sem("z_kept")
        dense_in = {zb: sem(f"dense_in{zb}") for zb in DENSE_BLOCKS}
        early_made = sem("early_made")
        early_kept = sem("early_kept")
        early_added = sem("early_added")
        h1_made = sem("h1_made")
        h1_added = sem("h1_added")
        h1_kept = sem("h1_kept")
        h2_made = sem("h2_made")
        h2_kept = sem("h2_kept")
        y_made = sem("y_made")
        y_kept = sem("y_kept")
        y_out = sem("y_out")

        mlp_loads = [(w1_sb, w1.rearrange("(k p) n -> p k n", p=P)),
                     (w2_sb, w2.rearrange("(k p) n -> p k n", p=P)),
                     (columns_sb[:, :], columns)]
        sums = [s for s in PLAN if s[0] == "sums"]
        sums_through = [next(i + 1 for i, s in enumerate(sums) if s[1] + s[2] >= TILE_BASE[g + 1])
                        for g in range(NGROUP)]
        chunk_last_group = [next(g for g in range(NGROUP)
                                 if PASS_BASE[g + 1] >= min(NPASS, (c + 1) * WCHUNK))
                            for c in range(NWCHUNK)]

        def w_lower(engine, c):
            engine.wait_ge(w_hi_made, c + 1)
            engine.tensor_tensor(w_lo[:, c, :].bitcast(F32R), w_lo[:, c, :], w_hi[:, c, :],
                                 ALU.subtract).then_inc(w_lo_made[c], 1)

        def table_rest(engine, h, i):
            of = slice(G * h, G * h + G)
            engine.wait_ge(part_made, SPLITS.index((h, i)) + 1)
            if i == 1:
                engine.wait_ge(rest_made[h], 1)
            engine.tensor_tensor(parts[2][0:HP, of, :] if i else tab[0:HP, of, :], tab[0:HP, of, :],
                                 parts[i][0:HP, of, :], ALU.subtract).then_inc(rest_made[h], 1)

        def wait_z(engine, zb):
            engine.wait_ge(z_kept, zb + 1)
            if zb in DENSE_BLOCKS:
                engine.wait_ge(dense_in[zb], 16 * sum(first // P == zb for first, _ in DENSE_ROWS))

        block = ctx.enter_context(nc.Block())

        @block.sync
        def _(sp):
            def load_tables(h):
                for n in range(G * h, G * h + G):
                    sp.dma_start(tab[0:HP, n, :], tables[HOT_FIELDS[n]].rearrange("(p c) d -> p (c d)", c=NSLICE))\
                        .then_inc(tab_in[h], 16)

            def load_ids(h):
                if h >= 2:
                    sp.wait_ge(ids_half_made, h - 1)
                sp.dma_start(ids_wide[h % 2], hot_ids[h:h + 1, :, :].broadcast_to([P, G, B]))\
                    .then_inc(ids_wide_in[h], 16)

            def load_w(c):
                sp.dma_start(w_lo[:, c, :], wst[c, :, :]).then_inc(w_in[c], 16)

            def fill_ring(c):
                sp.wait_ge(w_hi_made, c // G + 1)
                sp.wait_ge(w_lo_made[c // G], 1)
                if c >= WSLOTS:
                    sp.wait_ge(tiles_made, chunk_last_group[c - WSLOTS] + 1)
                q = K * (c % G)
                for i, part in enumerate((w_hi, w_hi, w_lo, w_lo)):
                    sp.dma_start(wring[K * i:K * i + K, c % WSLOTS, :, :].rearrange("p a b -> p (a b)"),
                                 part[q:q + K, c // G, :]).then_inc(wring_in[c % WSLOTS], 16)

            sp.dma_start(ids_sb[:, :], ids).then_inc(ids_in, 16)
            load_tables(0)
            load_ids(0)
            load_tables(1)
            load_ids(1)
            load_w(0)
            load_tables(2)
            load_ids(2)
            for c in range(1, NWCOL):
                load_w(c)
            ring_chunk = 0
            for step in PLAN:
                if ring_chunk < WSLOTS and step[0] == "stack":
                    fill_ring(ring_chunk)
                    ring_chunk += 1
                if step[0] == "stack":
                    J = step[1]
                    sp.wait_ge(stack_hi_made, turns(J))
                    sp.wait_ge(stack_lo_made, turns(J))
                    slot = J % STACKS
                    sp.dma_start(stack[P // 2:P, slot, 0:in_block(J), :],
                                 stack[0:P // 2, slot, 0:in_block(J), :]).then_inc(stacked[slot], 16)
                    if J == HOT_BLOCKS[-1]:
                        for h in range(NHOT):
                            sp.wait_ge(rest_made[h], 2)
                        sp.wait_ge(part_made, 2 * NHOT)
                        sp.wait_ge(hot_used, NHOT * NSLICE)
                        for dst, src in mlp_loads:
                            sp.dma_start(dst, src).then_inc(mlp_in, 16)
                elif step[0] == "z" and step[1] in DENSE_BLOCKS:
                    sp.wait_ge(z_kept, step[1] + 1)
                    for i, (first, row_step) in enumerate(DENSE_ROWS):
                        if first // P == step[1]:
                            p = first % P
                            sp.dma_start(z_sb[p:p + row_step + 1:row_step, step[1], :],
                                         dense_t[2 * i:2 * i + 2, :]).then_inc(dense_in[step[1]], 16)
                elif step[0] == "tiles":
                    while ring_chunk < NWCHUNK and chunk_last_group[ring_chunk - WSLOTS] <= step[1]:
                        fill_ring(ring_chunk)
                        ring_chunk += 1
            sp.wait_ge(y_kept, 1)
            sp.dma_start(y.rearrange("b o -> o b"), y_sb[:, :]).then_inc(y_out, 16)
            sp.wait_ge(y_out, 16)

        @block.gpsimd
        def _(pool):
            pool.memset(ident[:, :], 0.0).then_inc(consts_zero, 1)
            pool.memset(sel[:, :, :], 1.0).then_inc(consts_zero, 1)
            pool.iota(slice_rows_int[:, :], pattern=[[1, NSLICE]], base=0,
                      channel_multiplier=NSLICE).then_inc(rows_numbered, 1)
            pool.wait_ge(consts_zero, 2)
            pool.affine_select(out=ident[:, :], in_=ident[:, :], compare_op=ALU.not_equal, fill=1.0, base=0,
                               pattern=[[-1, P]], channel_multiplier=1).then_inc(consts_made, 1)
            pool.affine_select(out=sel[:, :, :], in_=sel[:, :, :], compare_op=ALU.is_ge, fill=0.0, base=0,
                               pattern=[[P, ZM], [-K, K]], channel_multiplier=1).then_inc(consts_made, 1)
            pool.wait_ge(consts_made, 2)
            pool.affine_select(out=sel[:, :, :], in_=sel[:, :, :], compare_op=ALU.is_ge, fill=0.0, base=K - 1,
                               pattern=[[-P, ZM], [K, K]], channel_multiplier=-1).then_inc(consts_made, 1)
            pool.wait_ge(ids_in, 16)
            for n, J in enumerate(GATHERED):
                if n >= GATHER_BUFS:
                    pool.wait_ge(turned, n - GATHER_BUFS + 1)
                for r in range(in_block(J)):
                    f = ORDER[G * J + r]
                    for b in range(NCHUNK):
                        pool.indirect_dma_start(
                            gathered[:, n % GATHER_BUFS, b, K * r:K * r + K], None, tables[f],
                            bass.IndirectOffsetOnAxis(ap=ids_sb[:, F * b + f:F * b + f + 1], axis=0),
                        ).then_inc(rows_in[J], 16)
                    work = POOL_WORK.get((J, r))
                    if work is not None and work[0] == "rest":
                        table_rest(pool, *work[1:])
                    elif work is not None:
                        w_lower(pool, work[1])
            for n in range(1, len(ROUNDS)):
                for i, m in enumerate(LAST_FIRST):
                    pool.wait_ge(early_kept, M1 * n + m + 1)
                    if n > 1:
                        pool.wait_ge(early_added, M1 * (n - 2) + i + 1)
                    pool.tensor_tensor(early_sum[0][m], early_sum[0][m], early_sum[n][m],
                                       ALU.add).then_inc(early_added, 1)

        @block.scalar
        def _(act):
            act.wait_ge(rows_numbered, 1)
            act.activation(slice_rows[:, :], slice_rows_int[:, :], ACT.Copy).then_inc(rows_made, 1)
            looked_up = 0
            for step in PLAN:
                if step[0] == "w_hi":
                    c = step[1]
                    act.wait_ge(w_in[c], 16)
                    act.activation(w_hi[:, c, :].bitcast(F32R), w_lo[:, c, :], ACT.Copy).then_inc(w_hi_made, 1)
                elif step[0] == "ids":
                    h = step[1]
                    act.wait_ge(ids_wide_in[h], 16)
                    if h >= 2:
                        act.wait_ge(hot_made, NSLICE * (h - 1))
                    act.activation(ids_half[h % 2], ids_wide[h % 2], ACT.Copy).then_inc(ids_half_made, 1)
                elif step[0] == "split":
                    J, i = step[1:]
                    of = slice(G * J, G * J + G)
                    if i == 0:
                        act.wait_ge(tab_in[J], 16 * G)
                    else:
                        act.wait_ge(rest_made[J], 1)
                    act.activation(parts[i][0:HP, of, :], tab[0:HP, of, :], ACT.Copy).then_inc(part_made, 1)
                elif step[0] == "keep":
                    J = step[1]
                    n = K * in_block(J)
                    for i in range(2):
                        if NBLK - G * (i + 1) <= J < NBLK - G * i:
                            act.wait_ge(ids_half_made, max(h for h in range(NHOT) if h % 2 == i) + 1)
                    if J in HOT_BLOCKS:
                        h = HOT_BLOCKS.index(J)
                        act.wait_ge(hot_used, NSLICE * (h + 1))
                        act.activation(eT[:, J, :], look_ps[h], ACT.Copy).then_inc(eT_made, 1)
                    else:
                        act.wait_ge(turned, GATHERED.index(J) + 1)
                        act.activation(eT[0:n, J, :], side_ps[0:n, :], ACT.Copy).then_inc(eT_made, 1)
                elif step[0] == "halve":
                    J = step[1]
                    n = K * in_block(J)
                    act.wait_ge(eT_made, turns(J))
                    slot = turns(J) % 2
                    if turns(J) > 2:
                        act.wait_ge(lo_made, turns(J) - 2)
                    act.activation(hi_lo[0:n, slot, 0, :].bitcast(F32R), eT[0:n, J, :],
                                   ACT.Copy).then_inc(hi_made, 1)
                    if J >= STACKS:
                        act.wait_ge(tiles_made, LAST_GROUP[J - STACKS] + 1)
                    for r in range(in_block(J)):
                        ins = act.activation(stack[0:K, J % STACKS, r, :].bitcast(F32R),
                                             eT[K * r:K * r + K, J, :], ACT.Copy)
                    ins.then_inc(stack_hi_made, 1)
                elif step[0] == "stack":
                    J = step[1]
                    act.wait_ge(lo_made, turns(J))
                    for r in range(in_block(J)):
                        ins = act.activation(stack[K:2 * K, J % STACKS, r, :].bitcast(F32R),
                                             hi_lo[K * r:K * r + K, turns(J) % 2, 1, :], ACT.Copy)
                    ins.then_inc(stack_lo_made, 1)
                elif step[0] == "z":
                    act.wait_ge(summed, step[2])
                    act.activation(z_sb[:, step[1], :], z_ps[:, :], ACT.Copy).then_inc(z_kept, 1)
                elif step[0] == "early" and step[3] == len(ROUNDS[step[2]]) - 1:
                    m, n = step[1:3]
                    act.wait_ge(early_made, M1 * n + m + 1)
                    if n == 0:
                        act.wait_ge(mlp_in, 16 * len(mlp_loads))
                        act.activation(early_sum[n][m], side_ps[:, :], ACT.Identity,
                                       bias=b1_sb[:, m:m + 1]).then_inc(early_kept, 1)
                    else:
                        for c in range(G * n - WSLOTS, G * n):
                            act.wait_ge(wring_in[c % WSLOTS], 16 * G * (c // WSLOTS + 1))
                        act.activation(early_sum[n][m], side_ps[:, :], ACT.Copy).then_inc(early_kept, 1)
            for i, m in enumerate(LAST_FIRST):
                act.wait_ge(h1_added, i + 1)
                act.activation(h1_sb[m], h1_sum[m], ACT.Relu).then_inc(h1_kept, 1)
            for m in range(M2):
                act.wait_ge(h2_made, m + 1)
                act.activation(h2_sb[m], h2_ps[m], ACT.Relu, bias=b2_sb[:, m:m + 1]).then_inc(h2_kept, 1)
            act.wait_ge(y_made, 1)
            act.activation(y_sb[:, :], y_ps, ACT.Copy).then_inc(y_kept, 1)

        @block.vector
        def _(dve):
            for step in PLAN:
                if step[0] == "w_lo":
                    w_lower(dve, step[1])
                elif step[0] == "rest":
                    table_rest(dve, *step[1:])
                elif step[0] == "look":
                    J, c0, c1 = step[1:]
                    if c0 == 0:
                        dve.wait_ge(rows_made, 1)
                        dve.wait_ge(ids_half_made, J + 1)
                    for c in range(c0, c1):
                        n = NSLICE * J + c
                        if n >= HOT_BUFS:
                            dve.wait_ge(hot_used, n - HOT_BUFS + 1)
                        dve.tensor_scalar(hot[n % HOT_BUFS][0:HP, :, :], ids_half[J % 2][0:HP, :, :],
                                          slice_rows[0:HP, c:c + 1], None, ALU.is_equal).then_inc(hot_made, 1)
                elif step[0] == "keep" and step[1] == NBLK - 1:
                    dve.memset(eT[K * in_block(NBLK - 1):P, NBLK - 1, :], 0.0).then_inc(pad_zeroed, 1)
                    dve.wait_ge(pad_zeroed, 1)
                elif step[0] == "halve":
                    J = step[1]
                    n = K * in_block(J)
                    dve.wait_ge(eT_made, turns(J))
                    dve.wait_ge(hi_made, turns(J))
                    slot = turns(J) % 2
                    if turns(J) > 2:
                        dve.wait_ge(stack_lo_made, turns(J) - 2)
                    dve.tensor_tensor(hi_lo[0:n, slot, 1, :].bitcast(F32R), eT[0:n, J, :],
                                      hi_lo[0:n, slot, 0, :], ALU.subtract).then_inc(lo_made, 1)
                elif step[0] == "tiles":
                    g = step[1]
                    J, I0, nI, tiles = GROUPS[g]
                    n = len(tiles)
                    dve.wait_ge(tiles_made, g + 1)
                    if g == FIRST_GROUP[J]:
                        dve.wait_ge(eT_made, max(turns(I) for I in range(J + 1)))
                    if g >= XSLOTS:
                        dve.wait_ge(summed, sums_through[g - XSLOTS])
                    if nI > 1:
                        field = eT[:, I0:I0 + n, :]
                    else:
                        field = eT[:, I0:I0 + 1, :].broadcast_to([P, n, B])
                    dve.tensor_tensor(prod[:, g % XSLOTS, 0:n, :], t_ps[g % 2][:, 0:n, :], field,
                                      ALU.mult).then_inc(multiplied, 1)
            for i, m in enumerate(LAST_FIRST):
                dve.wait_ge(h1_made, i + 1)
                dve.wait_ge(early_kept, m + 1)
                dve.wait_ge(early_added, M1 * (len(ROUNDS) - 2) + i + 1)
                if i == 0:
                    dve.wait_ge(summed, len(sums))
                dve.tensor_tensor(h1_sum[m], h1_ps[m], h_early[:, m, :], ALU.add).then_inc(h1_added, 1)

        @block.tensor
        def _(pe):
            passes = 0
            side_used = []

            def side_free():
                while side_used:
                    pe.wait_ge(*side_used.pop())

            pe.wait_ge(consts_made, 3)
            for step in PLAN:
                if step[0] == "look":
                    J, c0, c1 = step[1:]
                    if c0 == 0:
                        pe.wait_ge(rest_made[J], 2)
                    for c in range(c0, c1):
                        n = NSLICE * J + c
                        pe.wait_ge(hot_made, n + 1)
                        for i in range(3):
                            for r in range(G):
                                mm = pe.matmul(look_ps[J][K * r:K * r + K, :],
                                               parts[i][0:HP, G * J + r, K * c:K * c + K],
                                               hot[n % HOT_BUFS][0:HP, r, :],
                                               start=(c == 0 and i == 0), stop=(c == NSLICE - 1 and i == 2))
                        mm.then_inc(hot_used, 1)
                elif step[0] == "keep" and step[1] in GATHERED:
                    J = step[1]
                    n = K * in_block(J)
                    at = GATHERED.index(J) % GATHER_BUFS
                    pe.wait_ge(rows_in[J], 16 * in_block(J) * NCHUNK)
                    side_free()
                    for b in range(NCHUNK):
                        mm = pe.transpose(side_ps[0:n, P * b:P * b + P], gathered[:, at, b, 0:n], ident[:, :])
                    mm.then_inc(turned, 1)
                    side_used.append((eT_made, turns(J)))
                elif step[0] == "tiles":
                    g = step[1]
                    J, I0, nI, tiles = GROUPS[g]
                    if g == FIRST_GROUP[J]:
                        pe.wait_ge(stack_hi_made, turns(J))
                        pe.wait_ge(stack_lo_made, turns(J))
                        pe.wait_ge(stacked[J % STACKS], 16 * (J // STACKS + 1))
                    if g == 1:
                        pe.wait_ge(eT_made, 2)
                    if g >= 2:
                        pe.wait_ge(multiplied, g - 1)
                    for i, tile in enumerate(tiles):
                        for k, (src, _) in enumerate(tile):
                            c = passes // WCHUNK
                            if passes % WCHUNK == 0:
                                pe.wait_ge(wring_in[c % WSLOTS], 16 * G * (c // WSLOTS + 1))
                            mm = pe.matmul(t_ps[g % 2][:, i, :],
                                           wring[:, c % WSLOTS, passes % WCHUNK, :].bitcast(F32R),
                                           stack[:, J % STACKS, src - G * J, :].bitcast(F32R),
                                           start=(k == 0), stop=(k == len(tile) - 1))
                            passes += 1
                    mm.then_inc(tiles_made, 1)
                elif step[0] == "sums":
                    for t in range(step[1], step[1] + step[2]):
                        g = GROUP_OF_TILE[t]
                        u = t % ZTILES
                        if t == step[1] or g != GROUP_OF_TILE[t - 1]:
                            pe.wait_ge(multiplied, g + 1)
                        if t == 0:
                            pe.wait_ge(eT_made, NHOT)
                        elif u == 0:
                            pe.wait_ge(z_kept, t // ZTILES)
                        mm = pe.matmul(z_ps[K * (u % G):K * (u % G) + K, :], sel[:, u // G, :],
                                       prod[:, g % XSLOTS, t - TILE_BASE[g], :],
                                       start=(u < G), stop=(u >= ZTILES - G or t >= NTILE - G))
                    mm.then_inc(summed, 1)
                elif step[0] == "early":
                    m, n, i = step[1:]
                    cols = slice(P * m, P * m + P)
                    zb = ROUNDS[n][i]
                    if i == 0:
                        side_free()
                    if n == 0:
                        pe.wait_ge(mlp_in, 16 * len(mlp_loads))
                    wait_z(pe, zb)
                    w, x = w1_sb[:, zb, cols], z_sb[:, zb, :]
                    last = i == len(ROUNDS[n]) - 1
                    mm = pe.matmul(side_ps[:, :], w, x, start=(i == 0), stop=last)
                    if last:
                        mm.then_inc(early_made, 1)
                        side_used.append((early_kept, M1 * n + m + 1))
                elif step[0] == "long":
                    k = step[1]
                    if k == EARLY_Z:
                        side_free()
                    wait_z(pe, k)
                    pe.matmul(side_ps[:, :], w1_sb[:, k, H1 - P:H1], z_sb[:, k, :], start=(k == EARLY_Z), stop=False)
                elif step[0] == "late":
                    m, zb = step[1:]
                    if m == 0:
                        wait_z(pe, zb)
                        pe.wait_ge(multiplied, NGROUP - 1)
                    pe.matmul(h1_ps[m], w1_sb[:, zb, P * m:P * m + P], z_sb[:, zb, :],
                              start=(zb == EARLY_Z), stop=False)
            for i, m in enumerate(LAST_FIRST):
                if i == 0:
                    wait_z(pe, NZ - 1)
                pe.matmul(h1_ps[m], w1_sb[:, NZ - 1, P * m:P * m + P], z_sb[:, NZ - 1, :],
                          start=False, stop=True).then_inc(h1_made, 1)
            for i, k in enumerate(LAST_FIRST):
                pe.wait_ge(h1_kept, i + 1)
                if i == 0:
                    pe.wait_ge(multiplied, NGROUP)
                for m in range(M2):
                    mm = pe.matmul(h2_ps[m], w2_sb[:, k, P * m:P * m + P], h1_sb[k],
                                   start=(i == 0), stop=(i == M1 - 1))
                    if i == M1 - 1:
                        mm.then_inc(h2_made, 1)
            for k in range(M2):
                pe.wait_ge(h2_kept, k + 1)
                mm = pe.matmul(y_ps, w3_sb[:, k:k + 1], h2_sb[k], start=(k == 0), stop=(k == M2 - 1))
            mm.then_inc(y_made, 1)


def kernel(**inputs):
    import concourse.bacc as bacc
    from concourse.bass_utils import run_bass_kernel_spmd

    a = {k: np.asarray(v) for k, v in inputs.items()}
    wst, w1 = lay_out_weights(a["L0_rec_w"], a["W_top1"])
    arrays = {f"tbl_{f}": np.ascontiguousarray(a[f"tbl_{f}"]) for f in range(F)}
    arrays["ids"] = np.ascontiguousarray(a["ids"].reshape(NCHUNK, P, F).transpose(1, 0, 2).reshape(P, -1))
    arrays["hot_ids"] = np.ascontiguousarray(a["ids"].T[HOT_FIELDS].reshape(NHOT, G, B))
    arrays["dense_t"] = np.ascontiguousarray(a["dense_ctx"].T)
    arrays["wst"], arrays["w1"] = wst, w1
    arrays["w2"] = np.ascontiguousarray(a["W_top2"])
    arrays["columns"] = np.concatenate(
        [a[n].reshape(-1, P).T for n in ("b_top1", "b_top2", "W_top3")], axis=1)

    nc = bacc.Bacc("TRN2", target_bir_lowering=False, num_devices=1)
    ap = {name: nc.dram_tensor(name, v.shape, mybir.dt.from_np(v.dtype), kind="ExternalInput").ap()
          for name, v in arrays.items()}
    y = nc.dram_tensor("y", (B, 1), F32, kind="ExternalOutput").ap()
    dlrm_tower(nc, [ap[f"tbl_{f}"] for f in range(F)],
               *(ap[n] for n in ("ids", "hot_ids", "dense_t", "wst", "w1", "w2", "columns")), y)
    r = run_bass_kernel_spmd(nc, [arrays], core_ids=[0])
    return r.results[0]["y"]
```
